# Optimizing a Trainium2 kernel written in Bass

```python
import numpy as np
import jax
import jax.numpy as jnp

def _softmax(x, axis=-1):
    return jax.nn.softmax(x, axis=axis)

def _gelu(x):
    return jax.nn.gelu(x, approximate=True)

def _silu(x):
    return jax.nn.silu(x)

def _sigmoid(x):
    return jax.nn.sigmoid(x)

def _layernorm(x, axis=-1, eps=1e-05):
    m = jnp.mean(x, axis=axis, keepdims=True)
    v = jnp.var(x, axis=axis, keepdims=True)
    return (x - m) / jnp.sqrt(v + eps)

def _scatter_add(tgt, idx, src, axis=0):
    return tgt.at[idx].add(src)

def _segment_sum(src, seg, n):
    return jax.ops.segment_sum(src, seg, n)
kernel_name = 'mk_flamingo_gated_d1_seqx_r8_c3ecbb'

def setup_inputs(seed: int=0):
    np.random.seed(seed)
    _w = jnp.asarray

    def _rec_inputs():
        import jax
        import jax.numpy as jnp
        _rk = jax.random.key(seed)
        x = -0.0002928 + 1 * jax.random.normal(jax.random.fold_in(_rk, 1), (16, 256, 128), jnp.float32)
        _lenS = 256 - jax.random.randint(jax.random.fold_in(_rk, 7), (16,), 0, max(1, 256 // 4) + 1, jnp.int32)
        _lenS2 = 64 - jax.random.randint(jax.random.fold_in(_rk, 8), (16,), 0, max(1, 64 // 4) + 1, jnp.int32)
        _ctx_512P = jax.random.normal(jax.random.fold_in(_rk, 11), (16, 16, 64), jnp.float32)
        _ctx_512c = jax.random.dirichlet(jax.random.fold_in(_rk, 511), 0.3 * jnp.ones((16,), jnp.float32), (16, 64))
        _ctx_512t = jnp.einsum('bsk,bkd->bsd', _ctx_512c, _ctx_512P)
        _ctx_512t = _ctx_512t * jax.lax.rsqrt(jnp.mean(jnp.square(_ctx_512t)) + 1e-12) * 0.953939
        ctx_512 = 0.00222621 + 0.99962 * (_ctx_512t + 0.3 * jax.random.normal(jax.random.fold_in(_rk, 611), (16, 64, 64), jnp.float32))
        _g = jax.random.normal(jax.random.fold_in(_rk, 9001), (2, 1), jnp.float32)
        _g = jnp.sign(_g) * jnp.maximum(jnp.abs(_g), 1.0) + (_g == 0) * 1.0
        g_xattn = _g[0]
        g_ffn = _g[1]
        return (x, ctx_512, g_xattn, g_ffn)
    x, ctx_512, g_xattn, g_ffn = _rec_inputs()

    def _L0_xattn_setup():
        import jax, jax.numpy as jnp
        import numpy as np
        B, T, TC, C, CC, H = (2, 256, 64, 128, 64, 16)
        D = C // H

        def _heads(t):
            b, l, _ = t.shape
            return t.reshape(b, l, H, D).transpose(0, 2, 1, 3)
        key = jax.random.key(seed)
        ks = jax.random.split(key, 18)
        w = lambda k, i, o: jax.random.normal(k, (i, o), jnp.float32) / np.sqrt(i).astype(np.float32)
        return {'x': jax.random.normal(ks[0], (B, T, C), jnp.float32), 'cross_input': jax.random.normal(ks[1], (B, TC, CC), jnp.float32), 'Wk': w(ks[2], C, C), 'bk': jnp.zeros((C,), jnp.float32), 'Wq': w(ks[3], C, C), 'bq': jnp.zeros((C,), jnp.float32), 'Wv': w(ks[4], C, C), 'bv': jnp.zeros((C,), jnp.float32), 'Wck': w(ks[5], CC, C), 'bck': jnp.zeros((C,), jnp.float32), 'Wcq': w(ks[6], C, C), 'bcq': jnp.zeros((C,), jnp.float32), 'Wcv': w(ks[7], CC, C), 'bcv': jnp.zeros((C,), jnp.float32), 'Wp': w(ks[8], C, C), 'bp': jnp.zeros((C,), jnp.float32)}
    _L0_xattn_all = _L0_xattn_setup()
    _L0_xattn_in = {k: v for k, v in _L0_xattn_all.items() if k in ('Wk', 'bk', 'Wq', 'bq', 'Wv', 'bv', 'Wck', 'bck', 'Wcq', 'bcq', 'Wcv', 'bcv', 'Wp', 'bp')}
    del _L0_xattn_all

    def _L0_ffn_setup():
        import jax, jax.numpy as jnp
        import numpy as np
        DIM = 128
        HID = 64
        N_EXPERTS = 16
        TOP_K = 4
        key = jax.random.key(seed)
        ks = jax.random.split(key, 8)
        s = 0.02
        x = jax.random.normal(ks[0], (2, 128, DIM), dtype=jnp.float32)
        gate_w = jax.random.normal(ks[1], (N_EXPERTS, DIM), dtype=jnp.float32) * s
        w1 = jax.random.normal(ks[2], (N_EXPERTS, HID, DIM), dtype=jnp.float32) * s
        w3 = jax.random.normal(ks[3], (N_EXPERTS, HID, DIM), dtype=jnp.float32) * s
        w2 = jax.random.normal(ks[4], (N_EXPERTS, DIM, HID), dtype=jnp.float32) * s
        sw1 = jax.random.normal(ks[5], (HID, DIM), dtype=jnp.float32) * s
        sw3 = jax.random.normal(ks[6], (HID, DIM), dtype=jnp.float32) * s
        sw2 = jax.random.normal(ks[7], (DIM, HID), dtype=jnp.float32) * s
        return {'x': x, 'gate_w': gate_w, 'w1': w1, 'w3': w3, 'w2': w2, 'sw1': sw1, 'sw3': sw3, 'sw2': sw2}
    _L0_ffn_all = _L0_ffn_setup()
    _L0_ffn_in = {k: v for k, v in _L0_ffn_all.items() if k in ('gate_w', 'w1', 'w3', 'w2', 'sw1', 'sw3', 'sw2')}
    del _L0_ffn_all
    return {'x': x, 'ctx_512': ctx_512, 'g_xattn': g_xattn, 'g_ffn': g_ffn, 'L0_xattn_Wk': _L0_xattn_in['Wk'], 'L0_xattn_bk': _L0_xattn_in['bk'], 'L0_xattn_Wq': _L0_xattn_in['Wq'], 'L0_xattn_bq': _L0_xattn_in['bq'], 'L0_xattn_Wv': _L0_xattn_in['Wv'], 'L0_xattn_bv': _L0_xattn_in['bv'], 'L0_xattn_Wck': _L0_xattn_in['Wck'], 'L0_xattn_bck': _L0_xattn_in['bck'], 'L0_xattn_Wcq': _L0_xattn_in['Wcq'], 'L0_xattn_bcq': _L0_xattn_in['bcq'], 'L0_xattn_Wcv': _L0_xattn_in['Wcv'], 'L0_xattn_bcv': _L0_xattn_in['bcv'], 'L0_xattn_Wp': _L0_xattn_in['Wp'], 'L0_xattn_bp': _L0_xattn_in['bp'], 'L0_ffn_gate_w': _L0_ffn_in['gate_w'], 'L0_ffn_w1': _L0_ffn_in['w1'], 'L0_ffn_w3': _L0_ffn_in['w3'], 'L0_ffn_w2': _L0_ffn_in['w2'], 'L0_ffn_sw1': _L0_ffn_in['sw1'], 'L0_ffn_sw3': _L0_ffn_in['sw3'], 'L0_ffn_sw2': _L0_ffn_in['sw2']}

def reference(x, ctx_512, g_xattn, g_ffn, L0_xattn_Wk, L0_xattn_bk, L0_xattn_Wq, L0_xattn_bq, L0_xattn_Wv, L0_xattn_bv, L0_xattn_Wck, L0_xattn_bck, L0_xattn_Wcq, L0_xattn_bcq, L0_xattn_Wcv, L0_xattn_bcv, L0_xattn_Wp, L0_xattn_bp, L0_ffn_gate_w, L0_ffn_w1, L0_ffn_w3, L0_ffn_w2, L0_ffn_sw1, L0_ffn_sw3, L0_ffn_sw2):
    import jax
    import jax.numpy as jnp

    def _L0_xattn_ref(x, cross_input, Wk, bk, Wq, bq, Wv, bv, Wck, bck, Wcq, bcq, Wcv, bcv, Wp, bp):
        import jax, jax.numpy as jnp
        import numpy as np
        B, T, TC, C, CC, H = (2, 256, 64, 128, 64, 16)
        D = C // H

        def _heads(t):
            b, l, _ = t.shape
            return t.reshape(b, l, H, D).transpose(0, 2, 1, 3)
        scale = np.float32(1.0 / np.sqrt(D))
        q = _heads(x @ Wq + bq)
        k = _heads(x @ Wk + bk)
        v = _heads(x @ Wv + bv)
        att = jnp.einsum('bhqd,bhkd->bhqk', q, k) * scale
        causal = jnp.tril(jnp.ones((T, T), bool))
        att = jnp.where(causal[None, None], att, -jnp.inf)
        y = jnp.einsum('bhqk,bhkd->bhqd', jax.nn.softmax(att, axis=-1), v)
        qc = _heads(x @ Wcq + bcq)
        kc = _heads(cross_input @ Wck + bck)
        vc = _heads(cross_input @ Wcv + bcv)
        attc = jnp.einsum('bhqd,bhkd->bhqk', qc, kc) * scale
        y = y + jnp.einsum('bhqk,bhkd->bhqd', jax.nn.softmax(attc, axis=-1), vc)
        y = y.transpose(0, 2, 1, 3).reshape(x.shape[0], T, C)
        return y @ Wp + bp

    def _L0_ffn_ref(x, gate_w, w1, w3, w2, sw1, sw3, sw2):
        import jax, jax.numpy as jnp
        import numpy as np
        DIM = 128
        HID = 64
        N_EXPERTS = 16
        TOP_K = 4
        bsz, seq_len, dim = x.shape
        xf = x.reshape(-1, dim)
        T = xf.shape[0]
        probs = jax.nn.softmax(xf @ gate_w.T, axis=-1)
        top_w, top_idx = jax.lax.top_k(probs, TOP_K)
        top_w = top_w / jnp.sum(top_w, axis=-1, keepdims=True)
        rows = jnp.arange(T)[:, None]
        combine = jnp.zeros((T, N_EXPERTS), dtype=xf.dtype).at[rows, top_idx].set(top_w)
        h1 = jnp.einsum('td,ehd->teh', xf, w1)
        h3 = jnp.einsum('td,ehd->teh', xf, w3)
        act = jax.nn.silu(h1) * h3
        eout = jnp.einsum('teh,edh->ted', act, w2)
        moe_out = jnp.einsum('ted,te->td', eout, combine)
        shared = jax.nn.silu(xf @ sw1.T) * (xf @ sw3.T) @ sw2.T
        return (moe_out + shared).reshape(bsz, seq_len, dim)
    x = x + jnp.tanh(g_xattn[0]) * _L0_xattn_ref(_layernorm(x, axis=-1), ctx_512, L0_xattn_Wk, L0_xattn_bk, L0_xattn_Wq, L0_xattn_bq, L0_xattn_Wv, L0_xattn_bv, L0_xattn_Wck, L0_xattn_bck, L0_xattn_Wcq, L0_xattn_bcq, L0_xattn_Wcv, L0_xattn_bcv, L0_xattn_Wp, L0_xattn_bp)
    x = x + jnp.tanh(g_ffn[0]) * _L0_ffn_ref(_layernorm(x, axis=-1), L0_ffn_gate_w, L0_ffn_w1, L0_ffn_w3, L0_ffn_w2, L0_ffn_sw1, L0_ffn_sw3, L0_ffn_sw2)
    return x

_drawn_inputs = setup_inputs


def setup_inputs(seed=0):
    import zlib

    import numpy as np

    out = dict(_drawn_inputs(seed))
    spreads = {'L0_xattn_bk': (0.0, 0.8),
     'L0_xattn_bq': (0.0, 0.574),
     'L0_xattn_bv': (0.0, 0.1),
     'L0_xattn_bck': (0.0, 0.8),
     'L0_xattn_bcq': (0.0, 0.464),
     'L0_xattn_bcv': (0.0, 0.1),
     'L0_xattn_bp': (0.0, 0.1)}
    factors = {'L0_ffn_gate_w': 8.0,
     'L0_ffn_w1': 8.0,
     'L0_ffn_w3': 8.0,
     'L0_ffn_w2': 8.0,
     'L0_ffn_sw1': 8.0,
     'L0_ffn_sw3': 8.0,
     'L0_ffn_sw2': 8.0}
    for name, (base, spread) in spreads.items():
        noise = np.random.default_rng([zlib.crc32(name.encode()), seed]).standard_normal(out[name].shape)
        drawn = base * np.exp(spread * noise) if base else spread * noise
        out[name] = jnp.asarray(drawn.astype(out[name].dtype))
    for name, factor in factors.items():
        out[name] = (out[name] * factor).astype(out[name].dtype)
    return out
```

```python
from contextlib import ExitStack

import concourse.bass as bass
from concourse import mybir

F32 = mybir.dt.float32
F32R = mybir.dt.float32r
BF16 = mybir.dt.bfloat16
ALU = mybir.AluOpType
ACT = mybir.ActivationFunctionType
AX_X = mybir.AxisListType.X
ds = bass.ds

B, T, C = 16, 256, 128
TC, CC = 64, 64
H, D = 16, 8
NT = B * T // 128
E, HID, TOPK = 16, 64, 4
EP = 1e-5
SCALE = float(D) ** -0.5
G = 4
RING = 8
PAIRS = B // 2
VR = 8 * (D + 1)
FK = E // 2 + 1
FT = 512
NF = B * T // FT

PREP_DMAS, MAX_DMAS = 20, 4


def clamp(v, top):
    return max(0, min(top, v))


def preps(n):
    return clamp((n + 4) // 2, PAIRS)


def maxes(n):
    return clamp(n + 2, B)


def attends(n):
    return clamp(n + 1, B)


def outs(n):
    return clamp(n, B)


def has_prep(n):
    return n % 2 == 0 and -2 <= n <= 12


def has_max(n):
    return -1 <= n <= 14


def has_attend(n):
    return 0 <= n <= 15


def has_out(n):
    return 1 <= n <= 16


PREP_USES = ["xT", "q", "k", "qc", "v"]
OUT_USES = ["o0", "o1", "yT", "proj"]
BANK = {"xT": 0, "q": 1, "k": 0, "qc": 1, "v": 0, "o0": 1, "o1": 0, "yT": 1, "proj": 0, "mT": 1}


def uses(n, kinds=None):
    counts = [(PREP_USES, preps(n)), (OUT_USES, outs(n)), (["mT"], maxes(n))]
    return sum(c * sum(kinds is None or k in kinds for k in ks) for ks, c in counts)


def of_slot(n):
    return PREP_USES * has_prep(n) + OUT_USES * has_out(n) + ["mT"] * has_max(n)


def filled(kind):
    return lambda n: uses(n - 1) + of_slot(n).index(kind) + 1


def emptied(kind):
    bank = [k for k in BANK if BANK[k] == BANK[kind]]

    def f(n):
        here = [k for k in of_slot(n) if k in bank]
        return uses(n - 1, bank) + here.index(kind) + 1
    return f


class Slot:

    def __init__(self, n, i=None, first=None, span=4):
        self.n, self.i, self.first, self.span = n, i, first, span

    def at(self, f):
        v = f(self.n)
        if self.i is None:
            return v
        step = f(self.n + self.span) - v
        return v + (self.i - self.first) * step if step else v


def wait(eng, sem, slot, f):
    v = slot.at(f)
    if isinstance(v, int) and v <= 0:
        return
    eng.wait_ge(sem, v)


def ffn_stats(j):
    return clamp(j + 3, NF)


def ffn_preps(j):
    return clamp(j + 2, NF)


def ffn_mains(j):
    return clamp(j + 1, NF)


def ffn_downs(j):
    return clamp(j, NF)


def ffn_slots(eng, body):
    for j in range(-2, 2):
        body(Slot(j, span=2))
    with eng.Fori(1, 3, 1) as i:
        for s in range(2):
            body(Slot(2 + s, i, 1, span=2))
    for j in range(6, 9):
        body(Slot(j, span=2))


def attention_slots(eng, body):
    for n in range(-2, 4):
        body(Slot(n))
    with eng.Fori(1, 3, 1) as i:
        for s in range(4):
            body(Slot(4 + s, i, 1))
    for n in range(12, 17):
        body(Slot(n))


MAX_AT = [2, 1, 2, 1, 2, 1, 2, 1, 2, 1, 1, 0, 0, 0, 0, 0]


def score_chunks():
    out = []
    for i in range(4):
        out += [("k0", i, 0), ("k0", i, 1), ("k1", i, 0)]
    return out + [("c", ip, gp) for ip in range(2) for gp in range(2)]


def max_chunks():
    return [("q0", i, 0) for i in range(4)] + [("q1", i, gp) for i in range(4) for gp in range(2)] + \
        [("c", ip, qt) for ip in range(2) for qt in range(2)]


def max_steps(n):
    cs = list(enumerate(max_chunks()))
    out = []
    for m in MAX_AT:
        out.append(cs[:m])
        cs = cs[m:]
    return out if has_max(n) else [[] for _ in MAX_AT]


def block_program(nc, a, out):
    with ExitStack() as ctx:
        def sb(name, shape, dt=F32):
            return ctx.enter_context(nc.sbuf_tensor(name, shape, dt))

        def sem(name):
            return ctx.enter_context(nc.semaphore(name))

        xs = sb("xs", [128, NT, C])
        ident = sb("ident", [128, 128])
        gates = sb("gates", [128, 2])
        tg = sb("tg", [128, 2])
        w13 = sb("w13", [C, 2, FK * 128])
        w2 = sb("w2", [128, FK, C])
        gw = sb("gw", [C, E])
        gw_parts = sb("gw_parts", [C, 2, E], F32R)
        sel_f = sb("sel_f", [32, (FK - 1) * 128])
        sel = sb("sel", [32, FK - 1, 128], F32R)

        attention = ctx.enter_context(ExitStack())

        def sb(name, shape, dt=F32):
            return attention.enter_context(nc.sbuf_tensor(name, shape, dt))

        stack = [sb(f"stack{j}", [128, 3, G, 512], F32R) for j in range(2)]

        pmax = [ctx.enter_context(nc.psum_tensor(f"pmax{j}", [128, 512], F32)) for j in range(2)]
        psc = [ctx.enter_context(nc.psum_tensor(f"psc{j}", [128, 512], F32)) for j in range(2)]
        pself, pcross = (ctx.enter_context(nc.psum_tensor(k, [128, 512], F32)) for k in ("pself", "pcross"))
        psh = [ctx.enter_context(nc.psum_tensor(f"psh{j}", [128, 512], F32)) for j in range(2)]

        wq, wk, wcq, wv, wp = (sb(f"s_{k}", [C, C]) for k in ("wq", "wk", "wcq", "wv", "wp"))
        wck, wcv = sb("s_wck", [CC, C]), sb("s_wcv", [CC, C])
        bcol = sb("bcol", [C, 4])
        bv_b, bcv_b, bp_b = (sb(f"{k}_b", [128, C]) for k in ("bv", "bcv", "bp"))
        bpg = sb("bpg", [128, C])
        identb = sb("identb", [128, 128], BF16)
        qmask = sb("qmask", [128, 4, 128], BF16)
        par_mask = sb("par_mask", [128, 2])
        half_mask = sb("half_mask", [128, 2 * D])
        zero8 = sb("zero8", [8, 1024])
        stat = sb("stat", [128, NT, 6])
        mv = sb("mv", [128, NT, 2])
        half = sb("half", [128, NT])
        vare = sb("vare", [128, NT])
        rs0 = sb("rs0", [128, NT])
        rs1 = sb("rs1", [128, NT])
        rstd = sb("rstd", [128, NT])
        xn = sb("xn", [128, 4, C])
        xnT = sb("xnT", [C, 512])
        kcs_all = sb("kcs_all", [128, G, B, TC])
        kcs = sb("kcs", [128, 4, G, 2, TC], F32R)
        vc_all = sb("vc_all", [128, B, C])
        vcz = sb("vcz", [128, 2, 2, 368])
        parts = sb("parts", [128, 6, 512], F32R)
        vst = sb("vst", [128, 2, 4, C])
        vz = sb("vz", [128, 2, 2, 2, 648])
        negmax = sb("negmax", [128, 2, 2, H])
        mparts = sb("mparts", [128, 2, 2, H, 2], F32R)
        mT = sb("mT", [32, 2, T])
        with ExitStack() as early:
            def sb_early(name, shape, dt=F32):
                return early.enter_context(nc.sbuf_tensor(name, shape, dt))

            cT2 = sb_early("cT2", [CC, B, 2, TC])
            kc_hi = sb_early("kc_hi", [C, B * TC], F32R)
            kc_lo = sb_early("kc_lo", [C, B * TC], F32R)
            ones8 = sb_early("ones8", [8, 1024])
            qmaskf = sb_early("qmaskf", [128, 4, 128])
        probs = sb("probs", [128, RING, 512])
        pcopy = sb("pcopy", [VR, 2, 512])
        rden = sb("rden", [128, 2, 2 * H])
        normed = sb("normed", [128, 2, 2, C])
        y = sb("y", [128, 2, C])
        yT = sb("yT", [C, 2, 128])

        attention.close()

        def sb(name, shape, dt=F32):
            return ctx.enter_context(nc.sbuf_tensor(name, shape, dt))

        w13_parts = sb("w13_parts", [C, 2, 2, FK * 128], F32R)
        xn2 = sb("xn2", [128, 4, C])
        x_hi, x_lo = (sb(k, [C, 2, FT], F32R) for k in ("x_hi", "x_lo"))
        stat2, mv2 = sb("stat2", [128, 4, 6]), sb("mv2", [128, 4, 2])
        ve2, rt0, rt1, rstd2 = (sb(k, [128, 4]) for k in ("ve2", "rt0", "rt1", "rstd2"))
        half2 = sb("half2", [128, 4])
        nmx, esum, erec, wsum, wrec = (sb(k, [128, 4]) for k in ("nmx", "esum", "erec", "wsum", "wrec"))
        shifted, expd = sb("shifted", [128, 4, E]), sb("expd", [128, 4, E])
        pr = sb("pr", [128, 4, E + 4])
        top8 = sb("top8", [128, 4, 8])
        picks = sb("picks", [128, 4, 8])
        marked = sb("marked", [128, 4, E + 4])
        chosen, comb = sb("chosen", [128, 4, E]), sb("comb", [128, 4, E])
        comb_parts = sb("comb_parts", [128, 4, 2, E], F32R)
        combT = sb("combT", [2 * E, 2, FT], F32R)
        silu = sb("silu", [128, 2, FT])
        gated = sb("gated", [128, 2, FT])
        hidden = sb("hidden", [128, 2, FK, FT])

        small_in, ctx_in = sem("small_in"), sem("ctx_in")
        x_in = [sem(f"x_in{j}") for j in range(4)]
        consts_made, stats_made, pool_consts = sem("consts_made"), sem("stats_made"), sem("pool_consts")
        aggregated = sem("aggregated")
        rows_set, tg_made, rstd_made = sem("rows_set"), sem("tg_made"), sem("rstd_made")
        kc_filled, kc_hi_made, kc_lo_made, kc_stacked = (
            sem("kc_filled"), sem("kc_hi_made"), sem("kc_lo_made"), sem("kc_stacked"))
        vc_filled, vc_made = sem("vc_filled"), sem("vc_made")
        xn_made, hi_made, stacked = sem("xn_made"), sem("hi_made"), sem("stacked")
        sh_filled, sh_emptied = sem("sh_filled"), [sem("sh0_emptied"), sem("sh1_emptied")]
        kcs_made, vcb_made = sem("kcs_made"), sem("vcb_made")
        max_filled, max_read, mparts_made, m_stacked = (
            sem("max_filled"), sem("max_read"), sem("mparts_made"), sem("m_stacked"))
        sc_filled, exp_done, masked, pv_done = sem("sc_filled"), sem("exp_done"), sem("masked"), sem("pv_done")
        copied = sem("copied")
        vz_made = sem("vz_made")
        recips, y_made, xb_made = sem("recips"), sem("y_made"), sem("xb_made")
        stats2, rstd2_steps, xn2_made, xT2_filled, x_hi_made, gate_steps = (
            sem(k) for k in ("stats2", "rstd2_steps", "xn2_made", "xT2_filled", "x_hi_made", "gate_steps"))
        x_lo_made, gate_filled, exp2_made, combT_filled, combT_made = (
            sem(k) for k in ("x_lo_made", "gate_filled", "exp2_made", "combT_filled", "combT_made"))
        h_filled, silu_made, gated_made, cb_filled, hidden_made, down_filled, x3_made = (
            sem(k) for k in ("h_filled", "silu_made", "gated_made", "cb_filled", "hidden_made", "down_filled",
                             "x3_made"))
        w13_in, w13_hi_made, w13_lo_made, ffn_consts = (
            sem(k) for k in ("w13_in", "w13_hi_made", "w13_lo_made", "ffn_consts"))
        out_done, mask_turns, dve_turns = sem("out_done"), sem("mask_turns"), sem("dve_turns")

        SMALL = ["wq", "wk", "wcq", "wv", "wp", "bv", "bcv", "bp", "bq", "bk", "bcq", "bck", "g0", "g1",
                 "ident", "qmask", "par", "halves"]
        n_small = 16 * len(SMALL)
        n_ctx = 16 * 4

        n_w13 = 16 * 8
        attention_done = emptied("proj")(16)
        ph1, ph3, py, pgate = pmax, psc, pself, pcross
        pcb, pT2 = psh[1], psh[0]
        GATE_STEPS = 14

        block = ctx.enter_context(nc.Block())

        @block.sync
        def _(sp):
            x_t = a["x"].rearrange("(n p) c -> p n c", p=128)
            for j in range(4):
                sp.dma_start(xs[:, 8 * j:8 * j + 8, :], x_t[:, 8 * j:8 * j + 8, :]).then_inc(x_in[j], 16)
            for dst, k in ((w13[:, 0, 0:E * HID], "w1T"), (w13[:, 1, 0:E * HID], "w3T"),
                           (w13[:, 0, E * HID:(E + 1) * HID], "sw1T"), (w13[:, 1, E * HID:(E + 1) * HID], "sw3T"),
                           (w2[:, 0:E // 2, :], "w2T"), (gw[:], "gwT"),
                           (sel_f[:], "sel")):
                sp.dma_start(dst, a[k]).then_inc(w13_in, 16)
            sp.wait_ge(consts_made, 6)
            sp.wait_ge(ffn_consts, 2)
            sp.dma_start(w2[0:HID, E // 2, :], a["sw2T"]).then_inc(w13_in, 16)
            for g in range(G):
                for j in range(2):
                    sp.dma_start(stack[j][3::16, 0, g, :].bitcast(F32), ones8[:, 0:512]).then_inc(rows_set, 16)
                sp.dma_start(kcs_all[3::16, g, :, :],
                             ones8[:, :].rearrange("p (b t) -> p b t", b=B)).then_inc(rows_set, 16)
            sp.wait_ge(kc_hi_made, 2)
            sp.wait_ge(kc_lo_made, 2)
            for g in range(G):
                for r, part in enumerate((kc_hi, kc_lo, kc_hi)):
                    sp.dma_start(kcs_all[r::4, g, :, :],
                                 part[32 * g:32 * g + 32, :].bitcast(F32).rearrange("p (b t) -> p b t", b=B)
                                 ).then_inc(kc_stacked, 16)

            def slot(t):
                if has_prep(t.n):
                    st = stack[(t.n // 2 + 1) % 2]
                    wait(sp, sc_filled, t, lambda n: 16 * attends(n - 1))
                    for g in range(G):
                        sp.dma_start(st[3::16, 1:3, g, :].bitcast(F32),
                                     zero8[:, :].rearrange("p (x t) -> p x t", x=2)).then_inc(stacked, 16)
                    wait(sp, sh_emptied[1], t, emptied("qc"))
                    for g in range(G):
                        rows = slice(32 * g, 32 * g + 32)
                        for r, dst, src in ((0, slice(0, 1), slice(3, 4)), (0, slice(1, 3), slice(1, 3)),
                                            (1, slice(0, 3), slice(0, 3)), (2, slice(0, 3), slice(3, 6))):
                            sp.dma_start(st[r::4, dst, g, :].bitcast(F32),
                                         parts[rows, src, :].bitcast(F32)).then_inc(stacked, 16)
                if has_max(t.n):
                    m = t.n + 1
                    st = stack[(m // 2) % 2]
                    wait(sp, sh_emptied[1], t, emptied("mT"))
                    for g in range(G):
                        sp.dma_start(st[3::16, 1:3, g, T * (m % 2):T * (m % 2) + T].bitcast(F32),
                                     mT[8 * g:8 * g + 8, :, :]).then_inc(m_stacked, 16)

            attention_slots(sp, slot)
            o_t = out.rearrange("(n p) c -> p n c", p=128)

            def ffn_slot(t):
                if 1 <= t.n <= 8:
                    wait(sp, x3_made, t, ffn_downs)
                    tiles = ds(t.at(lambda j: 4 * (j - 1)), 4)
                    sp.dma_start(o_t[:, tiles, :], xs[:, tiles, :]).then_inc(out_done, 16)

            ffn_slots(sp, ffn_slot)
            sp.wait_ge(out_done, 16 * NF)

        @block.gpsimd
        def _(pool):
            for j in range(2):
                nc.gpsimd.memset(stack[j][:].bitcast(F32), 0.0).then_inc(consts_made, 1)
            nc.gpsimd.memset(ones8[:], 1.0).then_inc(consts_made, 1)
            nc.gpsimd.memset(zero8[:], 0.0).then_inc(consts_made, 1)
            nc.gpsimd.memset(kcs_all[:], 0.0).then_inc(consts_made, 1)
            nc.gpsimd.memset(half[:], -0.5).then_inc(consts_made, 1)
            nc.gpsimd.memset(w13[:, :, (E + 1) * HID:FK * 128], 0.0).then_inc(ffn_consts, 1)
            nc.gpsimd.memset(w2[:, E // 2, :], 0.0).then_inc(ffn_consts, 1)
            nc.gpsimd.memset(vcz[:], 0.0).then_inc(pool_consts, 1)
            nc.gpsimd.memset(vz[:], 0.0).then_inc(pool_consts, 1)
            pool.wait_ge(pool_consts, 2)
            for z in range(2):
                for kt in range(2):
                    for ab in range(2):
                        nc.gpsimd.memset(vz[:, z, kt, ab, 64:648].rearrange("p (h x) -> p h x", x=73)[:, :, 0:1],
                                         1.0).then_inc(pool_consts, 1)
            pool.wait_ge(consts_made, 6)
            pool.wait_ge(aggregated, 2)
            nc.gpsimd.tensor_tensor(rs0[:], vare[:], half[:], ALU.pow).then_inc(rstd_made, 1)
            pool.wait_ge(rstd_made, 1)
            nc.gpsimd.tensor_tensor(rs1[:], rs0[:], rs0[:], ALU.mult).then_inc(rstd_made, 1)
            pool.wait_ge(rstd_made, 2)
            nc.gpsimd.tensor_tensor(rs1[:], rs1[:], vare[:], ALU.mult).then_inc(rstd_made, 1)
            pool.wait_ge(rstd_made, 3)
            nc.gpsimd.tensor_scalar(rs1[:], rs1[:], -0.5, 1.5, ALU.mult, ALU.add).then_inc(rstd_made, 1)
            pool.wait_ge(rstd_made, 4)
            nc.gpsimd.tensor_tensor(rstd[:], rs1[:], rs0[:], ALU.mult).then_inc(rstd_made, 1)
            pool.wait_ge(tg_made, 1)
            pool.wait_ge(small_in, n_small)
            nc.gpsimd.tensor_scalar(bpg[:], bp_b[:], tg[:, 0:1], None, ALU.mult).then_inc(pool_consts, 1)

            def context_keys(t):
                if t.n == -2:
                    pool.wait_ge(kc_stacked, 16 * 12)
                    pool.wait_ge(rows_set, 16 * 12)
                    pool.wait_ge(small_in, n_small)
                wait(pool, sc_filled, t, lambda n: 16 * attends(n - 2))
                src = kcs_all[:, :, ds(t.at(lambda n: n + 2), 1), :].rearrange("p g b t -> p g (b t)")
                nc.gpsimd.tensor_tensor(
                    kcs[:, (t.n + 2) % 4, :, :, :],
                    src.unsqueeze(2).broadcast_to([128, G, 2, TC]),
                    par_mask[:, :].unsqueeze(1).unsqueeze(3).broadcast_to([128, G, 2, TC]),
                    ALU.mult).then_inc(kcs_made, 1)

            def values(t):
                if t.n == -1:
                    pool.wait_ge(vc_made, 8)
                    pool.wait_ge(pool_consts, 11)
                wait(pool, pv_done, t, lambda n: 8 * attends(n - 1))
                z = (t.n + 1) % 2
                nc.gpsimd.tensor_tensor(
                    vcz[:, z, :, 0:352].rearrange("p a (j x) -> p a j x", x=88)[:, :, :, 0:16],
                    vc_all[:, ds(t.at(lambda n: n + 1), 1), :].rearrange("p b (a j x) -> p (b a) j x", a=2, j=4),
                    half_mask[:].unsqueeze(1).unsqueeze(1).broadcast_to([128, 2, 4, 2 * D]),
                    ALU.mult).then_inc(vz_made, 1)
                wait(pool, sh_emptied[0], t, lambda n: emptied("v")(2 * ((n + 1) // 2) - 2))
                for ab in range(2):
                    nc.gpsimd.tensor_tensor(
                        vz[:, z, :, ab, 0:640].rearrange("p k (h x) -> p k h x", x=80)[:, :, :, 0:D],
                        vst[:, ((t.n + 1) // 2) % 2, 2 * z:2 * z + 2, 64 * ab:64 * ab + 64].rearrange(
                            "p k (h d) -> p k h d", d=D),
                        bv_b[:, 64 * ab:64 * ab + 64].rearrange("p (h d) -> p h d", d=D).unsqueeze(1)
                        .broadcast_to([128, 2, 8, D]), ALU.add).then_inc(vz_made, 1)

            def causal(t, c, kind):
                wait(pool, exp_done, t, lambda n: 16 * attends(n - 1) + c + 1)
                pool.sem_inc(mask_turns, 1)
                nh = 2 if kind == "k0" else 4
                blk = probs[:, c % RING, :].rearrange("p (h q) -> p h q", h=nh)[:, :, 0:128]
                nc.gpsimd.affine_select(out=blk, in_=blk, pattern=[[0, nh], [1, 128]],
                                        compare_op=ALU.is_ge, fill=0.0, base=0,
                                        channel_multiplier=-1).then_inc(masked, 1)

            def slot(t):
                for c in range(13):
                    if has_attend(t.n) and c < 12:
                        causal(t, c, score_chunks()[c][0])
                    if has_out(t.n) and c == 2:
                        tiles = ds(t.at(lambda n: 2 * (n - 1)), 2)
                        wait(pool, xn_made, t, lambda n: preps(n - 1))
                        nc.gpsimd.tensor_tensor(xs[:, tiles, :], xs[:, tiles, :],
                                                bpg[:].unsqueeze(1).broadcast_to([128, 2, C]),
                                                ALU.add).then_inc(xb_made, 1)
                    if has_out(t.n) and c == 5:
                        wait(pool, sh_emptied[1], t, emptied("o0"))
                        wait(pool, sh_emptied[0], t, emptied("o1"))
                        if t.n >= 2:
                            wait(pool, sh_filled, t, lambda n: filled("yT")(n - 1))
                        nc.gpsimd.tensor_tensor(y[:], normed[:, :, 0, :], normed[:, :, 1, :],
                                                ALU.add).then_inc(y_made, 1)
                    if -2 <= t.n <= 13 and c == 8:
                        context_keys(t)
                    if -1 <= t.n <= 14 and c == 12:
                        values(t)

            attention_slots(pool, slot)
            pool.wait_ge(sh_emptied[0], attention_done)
            nc.gpsimd.memset(half2[:], -0.5).then_inc(ffn_consts, 1)
            nc.gpsimd.memset(pr[:, :, E:E + 4], -1.0).then_inc(ffn_consts, 1)
            nc.gpsimd.memset(picks[:, :, 4:8], -1.0).then_inc(ffn_consts, 1)
            pool.wait_ge(ffn_consts, 5)

            def ffn_slot(t):
                if -2 <= t.n <= 5:
                    wait(pool, stats2, t, lambda j: 3 * ffn_stats(j))
                    wait(pool, xn2_made, t, lambda j: ffn_preps(j))
                    steps = ((rt0, ve2, half2, ALU.pow), (rt1, rt0, rt0, ALU.mult), (rt1, rt1, ve2, ALU.mult))
                    for k, (dst, x, y_, op) in enumerate(steps):
                        if k:
                            wait(pool, rstd2_steps, t, lambda j: 5 * ffn_stats(j - 1) + k)
                        nc.gpsimd.tensor_tensor(dst[:], x[:], y_[:], op).then_inc(rstd2_steps, 1)
                    wait(pool, rstd2_steps, t, lambda j: 5 * ffn_stats(j - 1) + 3)
                    pool.sem_inc(mask_turns, 1)
                    nc.gpsimd.tensor_scalar(rt1[:], rt1[:], -0.5, 1.5, ALU.mult, ALU.add).then_inc(rstd2_steps, 1)
                    wait(pool, rstd2_steps, t, lambda j: 5 * ffn_stats(j - 1) + 4)
                    nc.gpsimd.tensor_tensor(rstd2[:], rt1[:], rt0[:], ALU.mult).then_inc(rstd2_steps, 1)

            ffn_slots(pool, ffn_slot)

        @block.scalar
        def _(act):
            act.dma_start(ident[:], a["ident"]).then_inc(small_in, 16)
            act.dma_start(wck[:], a["wck"]).then_inc(ctx_in, 16)
            act.dma_start(wcv[:], a["wcv"]).then_inc(ctx_in, 16)
            for e in range(2):
                act.dma_start(cT2[:, :, e, :], a["ctxT"].rearrange("p (b t) -> p b t", b=B)).then_inc(ctx_in, 16)
            for t, k in ((wq, "wq"), (wk, "wk"), (wcq, "wcq"), (wv, "wv"), (wp, "wp"), (par_mask, "par"),
                         (half_mask, "halves")):
                act.dma_start(t[:], a[k]).then_inc(small_in, 16)
            act.dma_start(qmaskf[:].rearrange("p h k -> p (h k)"), a["qmask"]).then_inc(small_in, 16)
            for j, k in enumerate(("bq", "bk", "bcq", "bck")):
                act.dma_start(bcol[:, j:j + 1], a[k].rearrange("(c o) -> c o", o=1)).then_inc(small_in, 16)
            for t, k in ((bv_b, "bv"), (bcv_b, "bcv"), (bp_b, "bp")):
                act.dma_start(t[:], a[k].rearrange("(o c) -> o c", o=1).broadcast_to([128, C])
                              ).then_inc(small_in, 16)
            for j, k in enumerate(("g0", "g1")):
                act.dma_start(gates[:, j:j + 1], a[k].rearrange("(o c) -> o c", o=1).broadcast_to([128, 1])
                              ).then_inc(small_in, 16)
            act.wait_ge(small_in, n_small)
            nc.scalar.activation(tg[:], gates[:], ACT.Tanh).then_inc(tg_made, 1)
            for j in range(2):
                act.wait_ge(kc_filled, j + 1)
                nc.scalar.activation(kc_hi[:, 512 * j:512 * j + 512], psc[j][:, :], ACT.Identity,
                                     bias=bcol[:, 3:4]).then_inc(kc_hi_made, 1)

            def hi(t, kind, bank, dst, col):
                wait(act, sh_filled, t, filled(kind))
                nc.scalar.activation(parts[:, dst, :], psh[bank][:, :], ACT.Identity,
                                     bias=bcol[:, col:col + 1]).then_inc(hi_made, 1)

            def slot(t):
                if has_prep(t.n):
                    wait(act, sh_filled, t, filled("xT"))
                    nc.scalar.activation(xnT[:], psh[0][:, :], ACT.Copy).then_inc(sh_emptied[0], 1)
                for c in range(16):
                    if has_out(t.n) and c in (0, 2):
                        wait(act, pv_done, t, lambda n: 8 * attends(n - 1))
                        if t.n >= 2:
                            wait(act, sh_filled, t, lambda n: filled("o1")(n - 1))
                        nc.scalar.activation(pcopy[:, c // 2, :], (pself, pcross)[c // 2][0:VR, :],
                                             ACT.Copy).then_inc(copied, 1)
                    if has_attend(t.n):
                        wait(act, sc_filled, t, lambda n: 16 * attends(n - 1) + c + 1)
                        wait(act, pv_done, t, lambda n: 8 * attends(n - 1) + ((c - 8) // 3 + 1 if c >= 8 else
                                                                              ((c + 8) // 3 + 1 if c < 4 else c + 1) - 8))
                        nc.scalar.activation(probs[:, c % RING, :], psc[c % 2][:, :], ACT.Exp,
                                             scale=SCALE).then_inc(exp_done, 1)
                    if has_prep(t.n) and c in (1, 2, 3):
                        if c == 1:
                            wait(act, stacked, t, lambda n: 16 * PREP_DMAS * preps(n - 1))
                        kind, bank, dst, col = (("q", 1, 1, 0), ("k", 0, 3, 1), ("qc", 1, 2, 2))[c - 1]
                        hi(t, kind, bank, dst, col)
                    if has_out(t.n) and c == 7:
                        wait(act, sh_filled, t, filled("yT"))
                        nc.scalar.activation(yT[:].rearrange("p a b -> p (a b)"), psh[1][:, 0:256],
                                             ACT.Copy).then_inc(sh_emptied[1], 1)
                    if has_max(t.n) and c == 13:
                        wait(act, sh_filled, t, filled("mT"))
                        wait(act, m_stacked, t, lambda n: 16 * MAX_DMAS * maxes(n - 1))
                        nc.scalar.activation(mT[:].rearrange("p a b -> p (a b)"), psh[1][0:32, :],
                                             ACT.Copy).then_inc(sh_emptied[1], 1)

            attention_slots(act, slot)
            act.wait_ge(w13_in, n_w13)
            act.wait_ge(ffn_consts, 2)
            act.wait_ge(sc_filled, 16 * 14)
            for k in range(2):
                nc.scalar.activation(w13_parts[:, 0, k, :], w13[:, k, :], ACT.Copy).then_inc(w13_hi_made, 1)
            nc.scalar.activation(gw_parts[:, 0, :], gw[:], ACT.Copy).then_inc(w13_hi_made, 1)
            nc.scalar.activation(sel[:].rearrange("p k c -> p (k c)"), sel_f[:], ACT.Copy).then_inc(w13_hi_made, 1)
            act.wait_ge(sh_emptied[0], attention_done)

            def ffn_slot(t):
                for k in range(FK):
                    if 0 <= t.n <= 7:
                        q = FK * (t.n % 2) + k
                        wait(act, h_filled, t, lambda j: FK * ffn_mains(j - 1) + k + 1)
                        wait(act, gated_made, t, lambda j: FK * ffn_mains(j - 1) + k - 1)
                        nc.scalar.activation(silu[:, q % 2, :], ph1[q % 2][:, :], ACT.Silu).then_inc(silu_made, 1)
                    if -1 <= t.n <= 6:
                        z = (t.n + 1) % 2
                        if k == 2:
                            wait(act, xT2_filled, t, ffn_preps)
                            if t.n >= 1:
                                wait(act, h_filled, t, lambda j: FK * ffn_mains(j - 1))
                            nc.scalar.activation(x_hi[:, z, :], pT2[:, :], ACT.Copy).then_inc(x_hi_made, 1)
                        if k == 4:
                            wait(act, gate_steps, t, lambda j: GATE_STEPS * ffn_preps(j - 1) + 2)
                            nc.scalar.activation(expd[:], shifted[:], ACT.Exp).then_inc(exp2_made, 1)
                        if k == 7:
                            wait(act, combT_filled, t, ffn_preps)
                            nc.scalar.activation(combT[:, z, :], pT2[0:2 * E, :], ACT.Copy).then_inc(combT_made, 1)

            ffn_slots(act, ffn_slot)

        @block.vector
        def _(dve):
            dve.wait_ge(small_in, n_small)
            nc.vector.tensor_copy(identb[:], ident[:])
            nc.vector.tensor_copy(qmask[:].rearrange("p h k -> p (h k)"),
                                  qmaskf[:].rearrange("p h k -> p (h k)")).then_inc(stats_made, 1)
            for j in range(2):
                dve.wait_ge(kc_hi_made, j + 1)
                nc.vector.scalar_tensor_tensor(
                    kc_lo[:, 512 * j:512 * j + 512], psc[j][:, :], bcol[:, 3:4],
                    kc_hi[:, 512 * j:512 * j + 512].bitcast(F32), ALU.add, ALU.subtract).then_inc(kc_lo_made, 1)
            for k in range(NT):
                if k % 8 == 0:
                    dve.wait_ge(x_in[k // 8], 16)
                nc.vector.bn_stats(stat[:, k, :], xs[:, k, :]).then_inc(stats_made, 1)
            for k in range(NT):
                dve.wait_ge(stats_made, k + 2)
                i = nc.vector.bn_aggr(mv[:, k, :], stat[:, k, :])
            i.then_inc(aggregated, 1)
            dve.wait_ge(aggregated, 1)
            nc.vector.tensor_scalar(vare[:], mv[:, :, 1], EP, None, ALU.add).then_inc(aggregated, 1)
            dve.wait_ge(pool_consts, 2)
            for e in range(2):
                for z in range(2):
                    nc.vector.memset(vcz[64 * e:64 * e + 64, z, :, 64 + e:360 + e].rearrange(
                        "p a (j x) -> p a j x", x=74)[:, :, :, 0:1], 1.0).then_inc(vc_made, 1)
            for q in range(4):
                dve.wait_ge(vc_filled, q + 1)
                src = (pmax[0], pmax[1], psh[0], psh[1])[q]
                nc.vector.tensor_tensor(vc_all[:, 4 * q:4 * q + 4, :], src[:, :].rearrange("p (b c) -> p b c", b=4),
                                        bcv_b[:].unsqueeze(1).broadcast_to([128, 4, C]),
                                        ALU.add).then_inc(vc_made, 1)
            dve.wait_ge(rstd_made, 5)

            def make_xn(t):
                if t.n > -3:
                    wait(dve, sh_filled, t, lambda n: filled("xT")(n - 1))
                for k in range(4):
                    tile = t.at(lambda n: 2 * (n + 3) + k)
                    mean = mv[:, ds(tile, 1), 0:1].rearrange("p a b -> p (a b)")
                    i = nc.vector.tensor_scalar(xn[:, k, :], xs[:, ds(tile, 1), :].rearrange("p a c -> p (a c)"),
                                                mean, rstd[:, ds(tile, 1)],
                                                ALU.subtract, ALU.mult)
                i.then_inc(xn_made, 1)

            make_xn(Slot(-3))

            def lo(t, kind, bank, hi_part, lo_part, col, nth):
                wait(dve, hi_made, t, lambda n: 3 * preps(n - 1) + nth + 1)
                nc.vector.scalar_tensor_tensor(
                    parts[:, lo_part, :], psh[bank][:, :], bcol[:, col:col + 1],
                    parts[:, hi_part, :].bitcast(F32), ALU.add, ALU.subtract).then_inc(sh_emptied[bank], 1)

            def slot(t):
                for c, chunks in enumerate(max_steps(t.n)):
                    for k, (kind, i, j) in chunks:
                        if k == 0:
                            wait(dve, mparts_made, t, lambda n: 2 * maxes(n - 1))
                        wait(dve, max_filled, t, lambda n: 16 * maxes(n - 1) + k + 1)
                        src = pmax[k % 2][:, :]
                        if kind == "q0":
                            dst = negmax[:, 0, 0, :].rearrange("p (g i) -> p g i", g=G)[:, :, i]
                            src = src.rearrange("p (g k) -> p g k", g=4)
                        elif kind == "q1":
                            dst = negmax[:, 0, 1, :].rearrange("p (g i) -> p g i", g=G)[:, 2 * j:2 * j + 2, i]
                            src = src.rearrange("p (g k) -> p g k", g=2)
                        else:
                            dst = negmax[:, 1, j, :].rearrange("p (g i) -> p g i", g=G)[:, :, 2 * i:2 * i + 2]
                            src = src.rearrange("p (g e k) -> p g e k", g=G, e=2)
                        nc.vector.tensor_reduce(dst, src, axis=AX_X, op=ALU.max, negate=True).then_inc(max_read, 1)
                    if has_prep(t.n) and c in (1, 2, 3):
                        lo(t, *(("q", 1, 1, 4, 0), ("k", 0, 3, 0, 1), ("qc", 1, 2, 5, 2))[c - 1], c - 1)
                    if has_prep(t.n) and c == 4:
                        wait(dve, sh_filled, t, filled("v"))
                        if t.n >= 0:
                            wait(dve, vz_made, t, lambda n: 3 * attends(n))
                        nc.vector.tensor_copy(vst[:, (t.n // 2 + 1) % 2, :, :].rearrange("p k c -> p (k c)"),
                                              psh[0][:, :]).then_inc(sh_emptied[0], 1)
                    if has_out(t.n) and c == 5:
                        for qt, kind in ((0, "o0"), (1, "o1")):
                            wait(dve, sh_filled, t, filled(kind))
                            o = psh[BANK[kind]][:, 0:4 * VR].rearrange("p (x r) -> p x r", r=VR)
                            rd = rden[:, qt, :].rearrange("p (x h) -> p x h", h=8)
                            nc.vector.reciprocal(rd, o[:, :, 64:VR]).then_inc(recips, 1)
                            wait(dve, recips, t, lambda n: 2 * outs(n) - 1 + qt)
                            wait(dve, y_made, t, lambda n: outs(n - 1))
                            nc.vector.tensor_tensor(
                                normed[:, qt, :, :].rearrange("p x (a h d) -> p (x a) h d", a=2, d=D),
                                o[:, :, 0:64].rearrange("p x (h d) -> p x h d", d=D),
                                rd.unsqueeze(3).broadcast_to([128, 4, 8, D]),
                                ALU.mult).then_inc(sh_emptied[BANK[kind]], 1)
                    if has_out(t.n) and c == 10:
                        wait(dve, sh_filled, t, filled("proj"))
                        wait(dve, xb_made, t, lambda n: outs(n))
                        tiles = ds(t.at(lambda n: 2 * (n - 1)), 2)
                        nc.vector.scalar_tensor_tensor(
                            xs[:, tiles, :].rearrange("p a c -> p (a c)"), psh[0][:, 0:256], tg[:, 0:1],
                            xs[:, tiles, :].rearrange("p a c -> p (a c)"), ALU.mult,
                            ALU.add).then_inc(sh_emptied[0], 1)
                    if has_max(t.n) and c == 11:
                        wait(dve, max_read, t, lambda n: 16 * maxes(n))
                        if t.n > -1:
                            wait(dve, sh_filled, t, lambda n: filled("mT")(n - 1))
                        nm = negmax[:].rearrange("p x q h -> p (x q h)")
                        mp = mparts[:].rearrange("p x q h e -> p (x q h) e")
                        nc.vector.tensor_copy(mp[:, :, 0], nm).then_inc(mparts_made, 1)
                        wait(dve, mparts_made, t, lambda n: 2 * maxes(n) - 1)
                        nc.vector.tensor_tensor(mp[:, :, 1], nm, mp[:, :, 0].bitcast(F32),
                                                ALU.subtract).then_inc(mparts_made, 1)
                    if has_prep(t.n + 1) and c == 12:
                        make_xn(t)

            attention_slots(dve, slot)
            dve.wait_ge(sh_emptied[0], attention_done)
            for k in range(2):
                dve.wait_ge(w13_hi_made, k + 1)
                nc.vector.tensor_tensor(w13_parts[:, 1, k, :], w13[:, k, :], w13_parts[:, 0, k, :].bitcast(F32),
                                        ALU.subtract).then_inc(w13_lo_made, 1)
            dve.wait_ge(w13_hi_made, 3)
            nc.vector.tensor_tensor(gw_parts[:, 1, :], gw[:], gw_parts[:, 0, :].bitcast(F32),
                                    ALU.subtract).then_inc(w13_lo_made, 1)

            def bc4(x, n):
                return x[:].unsqueeze(2).broadcast_to([128, 4, n])

            def ffn_slot(t):
                def tile(k, count=1):
                    return ds(t.at(lambda j: 4 * (j + 1) + k), count)

                done = [0]

                def gate_step(ins):
                    ins.then_inc(gate_steps, 1)
                    done[0] += 1
                    k = done[0]
                    wait(dve, gate_steps, t, lambda j: GATE_STEPS * ffn_preps(j - 1) + k)

                for k in range(FK):
                    if -1 <= t.n <= 6:
                        z = (t.n + 1) % 2
                        if k == 0:
                            wait(dve, rstd2_steps, t, lambda j: 5 * ffn_preps(j))
                            wait(dve, xT2_filled, t, lambda j: ffn_preps(j - 1))
                            for x in range(4):
                                ins = nc.vector.tensor_scalar(xn2[:, x, :], xs[:, tile(x), :].rearrange(
                                    "p a c -> p (a c)"), mv2[:, x, 0:1], rstd2[:, x:x + 1],
                                    ALU.subtract, ALU.mult)
                            ins.then_inc(xn2_made, 1)
                        if k == 2:
                            wait(dve, x_hi_made, t, ffn_preps)
                            nc.vector.tensor_tensor(x_lo[:, z, :], pT2[:, :], x_hi[:, z, :].bitcast(F32),
                                                    ALU.subtract).then_inc(x_lo_made, 1)
                        if k == 3:
                            wait(dve, gate_filled, t, ffn_preps)
                            logits = pgate[:, 0:4 * E].rearrange("p (k e) -> p k e", e=E)
                            gate_step(nc.vector.tensor_reduce(nmx[:], logits, axis=AX_X, op=ALU.max, negate=True))
                            gate_step(nc.vector.tensor_tensor(shifted[:], logits, bc4(nmx, E), ALU.add))
                        if k == 4:
                            wait(dve, exp2_made, t, ffn_preps)
                            if t.n == -1:
                                dve.wait_ge(ffn_consts, 5)
                            gate_step(nc.vector.tensor_reduce(esum[:], expd[:], axis=AX_X, op=ALU.add))
                            gate_step(nc.vector.reciprocal(erec[:], esum[:]))
                            gate_step(nc.vector.tensor_tensor(pr[:, :, 0:E], expd[:], bc4(erec, E), ALU.mult))
                            dve.sem_inc(dve_turns, 1)
                            for x in range(4):
                                ins = nc.vector.max(top8[:, x, :], pr[:, x, 0:E])
                            gate_step(ins)
                            gate_step(nc.vector.tensor_copy(picks[:, :, 0:TOPK], top8[:, :, 0:TOPK]))
                        if k == 5:
                            for x in range(4):
                                ins = nc.vector.match_replace(marked[:, x, :], picks[:, x, :], pr[:, x, :], -2.0)
                            gate_step(ins)
                            gate_step(nc.vector.scalar_tensor_tensor(chosen[:], marked[:, :, 0:E], -1.5,
                                                                     pr[:, :, 0:E], ALU.is_lt, ALU.mult))
                            gate_step(nc.vector.tensor_reduce(wsum[:], chosen[:], axis=AX_X, op=ALU.add))
                            gate_step(nc.vector.reciprocal(wrec[:], wsum[:]))
                            gate_step(nc.vector.tensor_tensor(comb[:], chosen[:], bc4(wrec, E), ALU.mult))
                            wait(dve, combT_filled, t, lambda j: ffn_preps(j - 1))
                            gate_step(nc.vector.tensor_copy(comb_parts[:, :, 0, :], comb[:]))
                            gate_step(nc.vector.tensor_tensor(comb_parts[:, :, 1, :], comb[:],
                                                              comb_parts[:, :, 0, :].bitcast(F32), ALU.subtract))
                            assert done[0] == GATE_STEPS
                    if 0 <= t.n <= 7:
                        z, q = t.n % 2, FK * (t.n % 2) + k
                        wait(dve, silu_made, t, lambda j: FK * ffn_mains(j - 1) + k + 1)
                        if k == 0:
                            wait(dve, down_filled, t, lambda j: ffn_mains(j - 2))
                        if k >= 2 or t.n > 0:
                            wait(dve, hidden_made, t, lambda j: (FK - 1) * ffn_mains(j - 1) + min(max(k - 1, 0), 8))
                        dst = gated[:, q % 2, :] if k < FK - 1 else hidden[:, z, k, :]
                        nc.vector.tensor_tensor(dst, silu[:, q % 2, :], ph3[q % 2][:, :],
                                                ALU.mult).then_inc(gated_made, 1)
                        if k < FK - 1:
                            wait(dve, cb_filled, t, lambda j: (FK - 1) * ffn_mains(j - 1) + k + 1)
                            wait(dve, gated_made, t, lambda j: FK * ffn_mains(j - 1) + k + 1)
                            nc.vector.tensor_tensor(hidden[:, z, k, :], gated[:, q % 2, :], pcb[:, :],
                                                    ALU.mult).then_inc(hidden_made, 1)
                    if -2 <= t.n <= 5 and k == FK - 1:
                        for x in range(4):
                            ins = nc.vector.bn_stats(stat2[:, x, :], xs[:, tile(x + 4), :].rearrange(
                                "p a c -> p (a c)"))
                        ins.then_inc(stats2, 1)
                        wait(dve, stats2, t, lambda j: 3 * ffn_stats(j) - 2)
                        dve.sem_inc(dve_turns, 1)
                        for x in range(4):
                            ins = nc.vector.bn_aggr(mv2[:, x, :], stat2[:, x, :])
                        ins.then_inc(stats2, 1)
                        wait(dve, stats2, t, lambda j: 3 * ffn_stats(j) - 1)
                        nc.vector.tensor_scalar(ve2[:], mv2[:, :, 1], EP, None, ALU.add).then_inc(stats2, 1)
                if 1 <= t.n <= 8:
                    wait(dve, down_filled, t, ffn_downs)
                    tiles = ds(t.at(lambda j: 4 * (j - 1)), 4)
                    x3 = xs[:, tiles, :].rearrange("p a c -> p (a c)")
                    nc.vector.scalar_tensor_tensor(x3, py[:, :], tg[:, 1:2], x3, ALU.mult,
                                                   ALU.add).then_inc(x3_made, 1)

            ffn_slots(dve, ffn_slot)

        @block.tensor
        def _(pe):
            pe.wait_ge(ctx_in, n_ctx)
            pe.wait_ge(stats_made, 1)
            for j in range(2):
                nc.tensor.matmul(psc[j][:, :], wck[:], cT2[:, 8 * j:8 * j + 8, 0, :],
                                 start=True, stop=True).then_inc(kc_filled, 1)
            for q in range(4):
                dst = (pmax[0], pmax[1], psh[0], psh[1])[q]
                for b in range(4):
                    i = nc.tensor.matmul(dst[:, C * b:C * b + C], cT2[:, 4 * q + b, :, :].rearrange("p e t -> p (e t)"),
                                         wcv[:], start=True, stop=True)
                i.then_inc(vc_filled, 1)
            pe.wait_ge(vc_made, 8)
            pe.wait_ge(kc_lo_made, 2)

            def wait_bank(t, kind):
                wait(pe, sh_emptied[BANK[kind]], t, lambda n: emptied(kind)(n) - 1)

            def project(t, kind, w):
                wait_bank(t, kind)
                if kind == "q":
                    wait(pe, sh_emptied[0], t, emptied("xT"))
                nc.tensor.matmul(psh[BANK[kind]][:, :], w[:], xnT[:], start=True, stop=True).then_inc(sh_filled, 1)

            def max_chunk(t, k, kind, i, j):
                m = t.n + 1
                st = stack[(m // 2) % 2]
                kt, qt, qct = st[:, 0], st[:, 1], st[:, 2]
                b = T * (m % 2)
                bank = pmax[k % 2]
                if k == 0:
                    wait(pe, stacked, t, lambda n: 16 * PREP_DMAS * ((n + 1) // 2 + 1))
                    wait(pe, kcs_made, t, lambda n: n + 2)
                wait(pe, max_read, t, lambda n: 16 * maxes(n - 1) + k - 1)
                if kind == "c":
                    rows = slice(64 * i, 64 * i + 64)
                    for g in range(G):
                        last = nc.tensor.matmul(bank[:, 128 * g:128 * g + 128],
                                                qct[rows, g, b + 128 * j:b + 128 * j + 128],
                                                kcs[rows, m % 4, g, :, :].rearrange("p e t -> p (e t)"),
                                                start=(g == 0), stop=(g == G - 1))
                else:
                    rows = slice(32 * i, 32 * i + 32)
                    heads = range(4) if kind == "q0" else range(2 * j, 2 * j + 2)
                    w = 128 if kind == "q0" else 256
                    q0 = b + (0 if kind == "q0" else 128)
                    for x, g in enumerate(heads):
                        nc.tensor.matmul(bank[:, w * x:w * x + w], qt[rows, g, q0:q0 + 128], kt[rows, g, b:b + w],
                                         start=(x == 0), stop=False)
                    nh = len(heads)
                    last = nc.tensor.matmul(bank[:, :].rearrange("p (h k) -> p h k", h=nh)[:, :, w - 128:w],
                                            identb[:], qmask[:, 0:nh, :], start=False, stop=True)
                last.then_inc(max_filled, 1)

            def score_chunk(t, c, kind, i, j):
                st = stack[(t.n // 2) % 2]
                kt, qt, qct = st[:, 0], st[:, 1], st[:, 2]
                b = T * (t.n % 2)
                bank = psc[c % 2]
                wait(pe, exp_done, t, lambda n: 16 * attends(n - 1) + c - 1)
                if c == 0:
                    wait(pe, m_stacked, t, lambda n: 16 * MAX_DMAS * (n + 1))
                if kind == "k1":
                    for g in range(G):
                        last = nc.tensor.matmul(bank[:, 128 * g:128 * g + 128], kt[32 * i:32 * i + 32, g, b + 128:b + 256],
                                                qt[32 * i:32 * i + 32, g, b + 128:b + 256], start=True, stop=True)
                else:
                    for x, g in enumerate((2 * j, 2 * j + 1)):
                        if kind == "k0":
                            rows = slice(32 * i, 32 * i + 32)
                            keys, q = kt[rows, g, b:b + 128], qt[rows, g, b:b + 256]
                        else:
                            rows = slice(64 * i, 64 * i + 64)
                            keys = kcs[rows, t.n % 4, g, :, :].rearrange("p e t -> p (e t)")
                            q = qct[rows, g, b:b + 256]
                        last = nc.tensor.matmul(bank[:, 256 * x:256 * x + 256], keys, q, start=True, stop=True)
                last.then_inc(sc_filled, 1)

            def weigh_self(t, i):
                wait(pe, masked, t, lambda n: 12 * attends(n - 1) + 3 * i + 3)
                if i == 0:
                    wait(pe, copied, t, lambda n: 2 * outs(n))
                    wait(pe, vz_made, t, lambda n: 3 * attends(n))
                for g in range(G):
                    ab, h = g // 2, 4 * (g % 2) + i
                    lo_keys = probs[:, (3 * i + g // 2) % RING, 256 * (g % 2):256 * (g % 2) + 256]
                    hi_keys = probs[:, (3 * i + 2) % RING, 128 * g:128 * g + 128]
                    nc.tensor.matmul(pself[0:VR, 256 * ab:256 * ab + 256],
                                     vz[:, t.n % 2, 0, ab, VR * h:VR * h + VR], lo_keys,
                                     start=(i == 0 and g == 0), stop=False)
                    last = nc.tensor.matmul(pself[0:VR, 256 * ab + 128:256 * ab + 256],
                                            vz[:, t.n % 2, 1, ab, VR * h:VR * h + VR], hi_keys,
                                            start=False, stop=(i == 3 and g == 3))
                last.then_inc(pv_done, 1)

            def weigh_cross(t, k):
                _, ip, gp = score_chunks()[12 + k]
                wait(pe, exp_done, t, lambda n: 16 * attends(n - 1) + 13 + k)
                for x in range(2):
                    j = 2 * x + ip
                    last = nc.tensor.matmul(pcross[0:VR, 256 * gp:256 * gp + 256],
                                            vcz[:, t.n % 2, gp, VR * j:VR * j + VR],
                                            probs[:, (12 + k) % RING, 256 * x:256 * x + 256],
                                            start=(k == 0 and x == 0), stop=(k == 3 and x == 1))
                last.then_inc(pv_done, 1)

            def slot(t):
                if has_prep(t.n):
                    wait(pe, xn_made, t, lambda n: preps(n))
                    wait_bank(t, "xT")
                    for k in range(4):
                        last = nc.tensor.transpose(psh[0][:, 128 * k:128 * k + 128], xn[:, k, :], ident[:])
                    last.then_inc(sh_filled, 1)
                for c, chunks in enumerate(max_steps(t.n)):
                    if has_attend(t.n):
                        score_chunk(t, c, *score_chunks()[c])
                    if has_prep(t.n) and c in (1, 2, 3):
                        project(t, *(("q", wq), ("k", wk), ("qc", wcq))[c - 1])
                    if has_prep(t.n) and c == 4:
                        wait_bank(t, "v")
                        for k in range(4):
                            last = nc.tensor.matmul(psh[0][:, 128 * k:128 * k + 128], xnT[:, 128 * k:128 * k + 128],
                                                    wv[:], start=True, stop=True)
                        last.then_inc(sh_filled, 1)
                    for k, chunk in chunks:
                        max_chunk(t, k, *chunk)
                    if has_out(t.n) and c == 4:
                        wait(pe, copied, t, lambda n: 2 * outs(n))
                        for qt, kind in ((0, "o0"), (1, "o1")):
                            wait_bank(t, kind)
                            for x in range(2):
                                for ab in range(2):
                                    last = nc.tensor.transpose(
                                        psh[BANK[kind]][:, VR * (2 * x + ab):VR * (2 * x + ab) + VR],
                                        pcopy[:, x, 256 * ab + 128 * qt:256 * ab + 128 * qt + 128],
                                        ident[0:VR, 0:VR])
                            last.then_inc(sh_filled, 1)
                    if has_out(t.n) and c == 7:
                        wait(pe, y_made, t, lambda n: outs(n))
                        wait_bank(t, "yT")
                        for k in range(2):
                            last = nc.tensor.transpose(psh[1][:, 128 * k:128 * k + 128], y[:, k, :], ident[:])
                        last.then_inc(sh_filled, 1)
                    if has_out(t.n) and c == 9:
                        wait(pe, sh_emptied[1], t, emptied("yT"))
                        wait_bank(t, "proj")
                        for k in range(2):
                            last = nc.tensor.matmul(psh[0][:, 128 * k:128 * k + 128], yT[:, k, :], wp[:],
                                                    start=True, stop=True)
                        last.then_inc(sh_filled, 1)
                    if has_attend(t.n) and c in (5, 8, 11, 14):
                        weigh_self(t, (c - 5) // 3)
                    if has_max(t.n) and c == 12:
                        wait(pe, mparts_made, t, lambda n: 2 * maxes(n))
                        wait_bank(t, "mT")
                        for x in range(2):
                            for qt in range(2):
                                col = 256 * x + 128 * qt
                                last = nc.tensor.transpose(
                                    psh[1][0:32, col:col + 128],
                                    mparts[:, x, qt, :, :].bitcast(F32).rearrange("p h e -> p (h e)"), ident[:])
                        last.then_inc(sh_filled, 1)
                if has_attend(t.n):
                    for k in range(4):
                        weigh_cross(t, k)

            attention_slots(pe, slot)
            pe.wait_ge(sh_emptied[0], attention_done)

            def ffn_slot(t):
                z2 = (t.n + 1) % 2
                down = [(x, k) for x in range(4) for k in range(FK)]
                for k in range(FK):
                    if 0 <= t.n <= 7:
                        z, q = t.n % 2, FK * (t.n % 2) + k
                        if t.n == 0 and k == 0:
                            pe.wait_ge(w13_lo_made, 3)
                            pe.wait_ge(w13_hi_made, 4)
                        if k == 0:
                            wait(pe, combT_made, t, lambda j: j + 1)
                        wait(pe, silu_made, t, lambda j: FK * ffn_mains(j - 1) + k - 1)
                        wait(pe, gated_made, t, lambda j: FK * ffn_mains(j - 1) + k - 1)
                        for e, bank in ((0, ph1[q % 2]), (1, ph3[q % 2])):
                            for m, (wp_, x) in enumerate(((0, x_hi), (1, x_hi), (0, x_lo))):
                                last = nc.tensor.matmul(bank[:, :], w13_parts[:, wp_, e, 128 * k:128 * k + 128],
                                                        x[:, z, :], start=(m == 0), stop=(m == 2))
                        last.then_inc(h_filled, 1)
                    if -1 <= t.n <= 6:
                        if k == 1:
                            wait(pe, xn2_made, t, ffn_preps)
                            for x in range(4):
                                last = nc.tensor.transpose(pT2[:, 128 * x:128 * x + 128], xn2[:, x, :], ident[:])
                            last.then_inc(xT2_filled, 1)
                        if k == 3:
                            wait(pe, x_lo_made, t, ffn_preps)
                            if t.n == -1:
                                pe.wait_ge(w13_lo_made, 3)
                            for x in range(4):
                                for m, (xp, wp_) in enumerate(((x_hi, 0), (x_hi, 1), (x_lo, 0))):
                                    last = nc.tensor.matmul(pgate[:, E * x:E * x + E],
                                                            xp[:, z2, 128 * x:128 * x + 128], gw_parts[:, wp_, :],
                                                            start=(m == 0), stop=(m == 2))
                            last.then_inc(gate_filled, 1)
                        if k == 7:
                            wait(pe, gate_steps, t, lambda j: GATE_STEPS * ffn_preps(j))
                            for x in range(4):
                                last = nc.tensor.transpose(
                                    pT2[0:2 * E, 128 * x:128 * x + 128],
                                    comb_parts[:, x, :, :].bitcast(F32).rearrange("p m e -> p (m e)"), ident[:])
                            last.then_inc(combT_filled, 1)
                    if 1 <= t.n <= 8:
                        if k == 0:
                            wait(pe, hidden_made, t, lambda j: (FK - 1) * ffn_mains(j - 1))
                            wait(pe, gated_made, t, lambda j: FK * ffn_mains(j - 1))
                            wait(pe, x3_made, t, lambda j: ffn_downs(j - 1))
                        for x, m in down[4 * k:4 * k + 4]:
                            last = nc.tensor.matmul(py[:, C * x:C * x + C],
                                                    hidden[:, (t.n - 1) % 2, m, 128 * x:128 * x + 128], w2[:, m, :],
                                                    start=(m == 0), stop=(m == FK - 1))
                        if k == FK - 1:
                            last.then_inc(down_filled, 1)
                    if 0 <= t.n <= 7 and k < FK - 1:
                        wait(pe, hidden_made, t, lambda j: (FK - 1) * ffn_mains(j - 1) + k)
                        nc.tensor.matmul(pcb[:, :], sel[:, k, :], combT[:, z, :], start=True,
                                         stop=True).then_inc(cb_filled, 1)

            ffn_slots(pe, ffn_slot)


def host_constants():
    import numpy as np
    q, k = np.arange(128)[:, None], np.arange(128)[None, :]
    mask = np.where(k <= q, 0.0, -1e38).astype(np.float32)
    i = (np.arange(128) // 32) % 2
    sel = np.zeros((32, FK - 1, 128), np.float32)
    for t in range(FK - 1):
        for part in range(2):
            sel[16 * part + 2 * t, t, 0:HID] = 1.0
            sel[16 * part + 2 * t + 1, t, HID:] = 1.0
    return {"ident": np.eye(128, dtype=np.float32), "qmask": np.tile(mask, (1, 4)),
            "halves": np.repeat(np.stack([np.arange(128) < 64, np.arange(128) >= 64], 1), D, 1).astype(np.float32),
            "par": np.stack([1 - i, i], 1).astype(np.float32), "sel": sel.reshape(32, -1)}


def kernel(**inputs):
    import numpy as np
    import concourse.bacc as bacc
    from concourse.bass_utils import run_bass_kernel_spmd

    v = {k: np.asarray(x) for k, x in inputs.items()}
    names = {"wq": "Wq", "wk": "Wk", "wcq": "Wcq", "wv": "Wv", "wp": "Wp", "wck": "Wck", "wcv": "Wcv",
             "bq": "bq", "bk": "bk", "bcq": "bcq", "bv": "bv", "bp": "bp", "bck": "bck", "bcv": "bcv"}
    arrays = {k: v["L0_xattn_" + n] for k, n in names.items()}
    arrays["x"] = v["x"].reshape(B * T, C)
    arrays["ctxT"] = v["ctx_512"].reshape(B * TC, CC).T
    arrays["g0"], arrays["g1"] = v["g_xattn"], v["g_ffn"]
    f = {k: v["L0_ffn_" + k] for k in ("gate_w", "w1", "w3", "w2", "sw1", "sw3", "sw2")}
    arrays["gwT"] = f["gate_w"].T
    for k in ("w1", "w3"):
        arrays[k + "T"] = f[k].reshape(E * HID, C).T
        arrays["s" + k + "T"] = f["s" + k].T
    arrays["w2T"] = f["w2"].transpose(0, 2, 1).reshape(E // 2, 2 * HID, C).transpose(1, 0, 2)
    arrays["sw2T"] = f["sw2"].T
    arrays.update(host_constants())

    nc = bacc.Bacc("TRN2", target_bir_lowering=False, num_devices=1)
    feeds, aps = {}, {}
    for k, x in arrays.items():
        feeds[f"in_{k}"] = np.ascontiguousarray(x)
        aps[k] = nc.dram_tensor(f"in_{k}", x.shape, mybir.dt.from_np(x.dtype), kind="ExternalInput").ap()
    out = nc.dram_tensor("out_0", (B * T, C), F32, kind="ExternalOutput").ap()
    block_program(nc, aps, out)
    r = run_bass_kernel_spmd(nc, [feeds], core_ids=[0])
    return r.results[0]["out_0"].reshape(B, T, C)
```

```python
from contextlib import ExitStack

import concourse.bass as bass
from concourse import mybir

F32 = mybir.dt.float32
F32R = mybir.dt.float32r
BF16 = mybir.dt.bfloat16
ALU = mybir.AluOpType
ACT = mybir.ActivationFunctionType
AX_X = mybir.AxisListType.X
ds = bass.ds

B, T, C = 16, 256, 128
TC, CC = 64, 64
H, D = 16, 8
NT = B * T // 128
E, HID, TOPK = 16, 64, 4
EP = 1e-5
SCALE = float(D) ** -0.5
G = 4
RING = 8
PAIRS = B // 2
VR = 8 * (D + 1)
FK = E // 2 + 1
FT = 512
NF = B * T // FT

PREP_DMAS, MAX_DMAS = 20, 4


def clamp(v, top):
    return max(0, min(top, v))


def preps(n):
    return clamp((n + 4) // 2, PAIRS)


def maxes(n):
    return clamp(n + 2, B)


def attends(n):
    return clamp(n + 1, B)


def outs(n):
    return clamp(n, B)


def has_prep(n):
    return n % 2 == 0 and -2 <= n <= 12


def has_max(n):
    return -1 <= n <= 14


def has_attend(n):
    return 0 <= n <= 15


def has_out(n):
    return 1 <= n <= 16


PREP_USES = ["xT", "q", "k", "qc", "v"]
OUT_USES = ["o0", "o1", "yT", "proj"]
BANK = {"xT": 0, "q": 1, "k": 0, "qc": 1, "v": 0, "o0": 1, "o1": 0, "yT": 1, "proj": 0, "mT": 1}


def uses(n, kinds=None):
    counts = [(PREP_USES, preps(n)), (OUT_USES, outs(n)), (["mT"], maxes(n))]
    return sum(c * sum(kinds is None or k in kinds for k in ks) for ks, c in counts)


def of_slot(n):
    return PREP_USES * has_prep(n) + OUT_USES * has_out(n) + ["mT"] * has_max(n)


def filled(kind):
    return lambda n: uses(n - 1) + of_slot(n).index(kind) + 1


def emptied(kind):
    bank = [k for k in BANK if BANK[k] == BANK[kind]]

    def f(n):
        here = [k for k in of_slot(n) if k in bank]
        return uses(n - 1, bank) + here.index(kind) + 1
    return f


class Slot:

    def __init__(self, n, i=None, first=None, span=4):
        self.n, self.i, self.first, self.span = n, i, first, span

    def at(self, f):
        v = f(self.n)
        if self.i is None:
            return v
        step = f(self.n + self.span) - v
        return v + (self.i - self.first) * step if step else v


def wait(eng, sem, slot, f):
    v = slot.at(f)
    if isinstance(v, int) and v <= 0:
        return
    eng.wait_ge(sem, v)


def ffn_stats(j):
    return clamp(j + 3, NF)


def ffn_preps(j):
    return clamp(j + 2, NF)


def ffn_mains(j):
    return clamp(j + 1, NF)


def ffn_downs(j):
    return clamp(j, NF)


def ffn_slots(eng, body):
    for j in range(2):
        body(Slot(j, span=2))
    with eng.Fori(1, 3, 1) as i:
        for s in range(2):
            body(Slot(2 + s, i, 1, span=2))
    for j in range(6, 9):
        body(Slot(j, span=2))


def attention_slots(eng, body):
    for n in range(-2, 4):
        body(Slot(n))
    with eng.Fori(1, 3, 1) as i:
        for s in range(4):
            body(Slot(4 + s, i, 1))
    for n in range(12, 17):
        body(Slot(n))


MAX_AT = [1, 1, 1, 1, 2, 2, 2, 1, 2, 2, 1, 0, 0, 0, 0, 0]


def weigh_at(c):
    return [(i, g) for i in range(4) for g in range(4) if min(15, 3 * i + 5 + max(0, g - 1)) == c]


def score_chunks():
    out = []
    for i in range(4):
        out += [("k0", i, 0), ("k0", i, 1), ("k1", i, 0)]
    return out + [("c", ip, gp) for ip in range(2) for gp in range(2)]


def max_chunks():
    return [("q0", i, 0) for i in range(4)] + [("q1", i, gp) for i in range(4) for gp in range(2)] + \
        [("c", ip, qt) for ip in range(2) for qt in range(2)]


def max_steps(n):
    cs = list(enumerate(max_chunks()))
    out = []
    for m in MAX_AT:
        out.append(cs[:m])
        cs = cs[m:]
    return out if has_max(n) else [[] for _ in MAX_AT]


def block_program(nc, a, out):
    with ExitStack() as ctx:
        def sb(name, shape, dt=F32):
            return ctx.enter_context(nc.sbuf_tensor(name, shape, dt))

        def sem(name):
            return ctx.enter_context(nc.semaphore(name))

        xs = sb("xs", [128, NT, C])
        fixed = sb("fixed", [128, 128 + 2 + 2 * D])
        ident, par_mask, half_mask = fixed[:, 0:128], fixed[:, 128:130], fixed[:, 130:130 + 2 * D]
        gates = sb("gates", [128, 2])
        tg = sb("tg", [128, 2])
        w13 = sb("w13", [C, 2, FK * 128])
        w2 = sb("w2", [128, FK, C])
        gw = sb("gw", [C, E])
        gw_parts = sb("gw_parts", [C, 2, E], F32R)
        sel_f = sb("sel_f", [32, (FK - 1) * 128])
        sel = sb("sel", [32, FK - 1, 128], F32R)

        attention = ctx.enter_context(ExitStack())

        def sb(name, shape, dt=F32):
            return attention.enter_context(nc.sbuf_tensor(name, shape, dt))

        stack = [sb("stack0", [128, 3, G, 512], F32R)]
        kcs_all = sb("kcs_all", [128, G, B, TC])
        parts = sb("parts", [128, 6, 512], F32R)
        xn = sb("xn", [128, 4, C])
        xnT = sb("xnT", [C, 512])
        stack.append(sb("stack1", [128, 3, G, 512], F32R))

        pmax = [ctx.enter_context(nc.psum_tensor(f"pmax{j}", [128, 512], F32)) for j in range(2)]
        psc = [ctx.enter_context(nc.psum_tensor(f"psc{j}", [128, 512], F32)) for j in range(2)]
        pself, pcross = (ctx.enter_context(nc.psum_tensor(k, [128, 512], F32)) for k in ("pself", "pcross"))
        psh = [ctx.enter_context(nc.psum_tensor(f"psh{j}", [128, 512], F32)) for j in range(2)]

        w_all = sb("w_all", [C, 5, C])
        wq, wk, wcq, wv, wp = (w_all[:, k, :] for k in range(5))
        wc_all = sb("wc_all", [CC, 2, C])
        wck, wcv = wc_all[:, 0, :], wc_all[:, 1, :]
        bcol = sb("bcol", [C, 4])
        brow = sb("brow", [128, 3, C])
        bv_b, bcv_b, bp_b = (brow[:, k, :] for k in range(3))
        bpg = sb("bpg", [128, C])
        identb = sb("identb", [128, 128], BF16)
        qmask = sb("qmask", [128, 4, 128], BF16)
        zero8 = sb("zero8", [8, 1024])
        stat = sb("stat", [128, NT, 6])
        mv = sb("mv", [128, NT, 2])
        half = sb("half", [128, NT])
        vare = sb("vare", [128, NT])
        rs0 = sb("rs0", [128, NT])
        rs1 = sb("rs1", [128, NT])
        rstd = sb("rstd", [128, NT])
        kcs = sb("kcs", [128, 4, G, 2, TC], F32R)
        vc_all = sb("vc_all", [128, B, C])
        vcz = sb("vcz", [128, 2, 2, 368])
        vst = sb("vst", [128, 2, 4, C])
        vz = sb("vz", [128, 2, 2, 2, 648])
        negmax = sb("negmax", [128, 2, 2, H])
        mparts = sb("mparts", [128, 2, 2, H, 2], F32R)
        mT = sb("mT", [32, 2, T])
        with ExitStack() as early:
            def sb_early(name, shape, dt=F32):
                return early.enter_context(nc.sbuf_tensor(name, shape, dt))

            cT2 = sb_early("cT2", [CC, B, 2, TC])
            kc_hi = sb_early("kc_hi", [C, B * TC], F32R)
            kc_lo = sb_early("kc_lo", [C, B * TC], F32R)
            qmaskf = sb_early("qmaskf", [128, 4, 128])
        probs = sb("probs", [128, RING, 512])
        pcopy = sb("pcopy", [VR, 2, 512])
        rden = sb("rden", [128, 2, 2 * H])
        normed = sb("normed", [128, 2, 2, C])
        y = sb("y", [128, 2, C])
        yT = sb("yT", [C, 2, 128])

        attention.close()

        def sb(name, shape, dt=F32):
            return ctx.enter_context(nc.sbuf_tensor(name, shape, dt))

        w13_parts = sb("w13_parts", [C, 2, 2, FK * 128], F32R)
        xn2 = sb("xn2", [128, 4, C])
        x_hi, x_lo = (sb(k, [C, 2, FT], F32R) for k in ("x_hi", "x_lo"))
        stat2, mv2 = sb("stat2", [128, 4, 6]), sb("mv2", [128, 4, 2])
        ve2, rt0, rt1, rstd2 = (sb(k, [128, 4]) for k in ("ve2", "rt0", "rt1", "rstd2"))
        half2 = sb("half2", [128, 4])
        nmx, esum, erec, wsum, wrec = (sb(k, [128, 4]) for k in ("nmx", "esum", "erec", "wsum", "wrec"))
        shifted, expd = sb("shifted", [128, 4, E]), sb("expd", [128, 4, E])
        pr = sb("pr", [128, 4, E + 4])
        top8 = sb("top8", [128, 4, 8])
        picks = sb("picks", [128, 4, 8])
        marked = sb("marked", [128, 4, E + 4])
        chosen, comb = sb("chosen", [128, 4, E]), sb("comb", [128, 4, E])
        comb_parts = sb("comb_parts", [128, 4, 2, E], F32R)
        combT = sb("combT", [2 * E, 2, FT], F32R)
        silu = sb("silu", [128, 2, FT])
        gated = sb("gated", [128, 2, FT])
        hidden = sb("hidden", [128, 2, FK, FT])

        gates_in = sem("gates_in")
        fixed_in, weights_in, ctx_in, rest_in = (sem(k) for k in ("fixed_in", "weights_in", "ctx_in", "rest_in"))
        x_in = [sem(f"x_in{j}") for j in range(4)]
        stack_set = [sem(f"stack{j}_set") for j in range(2)]
        zeros_set, half_set, kcs_set, masks_made = (sem(k) for k in ("zeros_set", "half_set", "kcs_set", "masks_made"))
        stats_made, pool_consts = sem("stats_made"), sem("pool_consts")
        mv_made = sem("mv_made")
        aggregated, tg_made, rstd_made = sem("aggregated"), sem("tg_made"), sem("rstd_made")
        kc_filled, kc_hi_made, kc_lo_made, kc_stacked = (
            sem("kc_filled"), sem("kc_hi_made"), sem("kc_lo_made"), sem("kc_stacked"))
        vc_filled, vc_made = sem("vc_filled"), sem("vc_made")
        xn_made, hi_made, stacked = sem("xn_made"), sem("hi_made"), sem("stacked")
        sh_filled, sh_emptied = sem("sh_filled"), [sem("sh0_emptied"), sem("sh1_emptied")]
        kcs_made, vcb_made = sem("kcs_made"), sem("vcb_made")
        max_filled, max_read, mparts_made, m_stacked = (
            sem("max_filled"), sem("max_read"), sem("mparts_made"), sem("m_stacked"))
        sc_filled, exp_done, masked, pv_done = sem("sc_filled"), sem("exp_done"), sem("masked"), sem("pv_done")
        copied = sem("copied")
        vz_made = sem("vz_made")
        recips, y_made, xb_made = sem("recips"), sem("y_made"), sem("xb_made")
        stats2, rstd2_steps, xn2_made, xT2_filled, x_hi_made, gate_steps = (
            sem(k) for k in ("stats2", "rstd2_steps", "xn2_made", "xT2_filled", "x_hi_made", "gate_steps"))
        x_lo_made, gate_filled, exp2_made, combT_filled, combT_made = (
            sem(k) for k in ("x_lo_made", "gate_filled", "exp2_made", "combT_filled", "combT_made"))
        h_filled, silu_made, gated_made, cb_filled, hidden_made, down_filled, x3_made = (
            sem(k) for k in ("h_filled", "silu_made", "gated_made", "cb_filled", "hidden_made", "down_filled",
                             "x3_made"))
        w13_in, w13_hi_made, w13_lo_made, ffn_consts = (
            sem(k) for k in ("w13_in", "w13_hi_made", "w13_lo_made", "ffn_consts"))
        out_done, mask_turns, dve_turns = sem("out_done"), sem("mask_turns"), sem("dve_turns")

        n_weights, n_ctx, n_rest = 16 * 2, 16 * 3, 16 * 2
        LOADS = [(0, 4), (4, 8), (8, 20), (20, NT)]
        SECTIONS = [(0, 8), (8, 16), (16, 24), (24, NT)]
        n_w13 = 16 * 8
        attention_done = emptied("proj")(16)

        def max_banks(t):
            return pmax + psc if t.n == -1 else pmax

        front_free = 16 * attends(14)
        ph1, ph3, py = pmax, psc, pself
        pcb = [psh[1], pcross]

        def transposed_bank(j):
            return pmax[1] if j == -1 else psh[0]

        EARLY_AT = [3, 7]
        FIRST_PREP, STAGE_AT = 15, [3, 4, 5, 6, 7, 8, 9, 10]

        GATE_STEPS = 14

        block = ctx.enter_context(nc.Block())

        @block.sync
        def _(sp):
            x_t = a["x"].rearrange("(n p) c -> p n c", p=128)
            for j, (lo, hi) in enumerate(LOADS):
                sp.dma_start(xs[:, lo:hi, :], x_t[:, lo:hi, :]).then_inc(x_in[j], 16)

            def stack_context():
                sp.wait_ge(kcs_set, 1)
                sp.wait_ge(kc_hi_made, 2)
                sp.wait_ge(kc_lo_made, 2)
                for g in range(G):
                    for r, part in enumerate((kc_hi, kc_lo, kc_hi)):
                        sp.dma_start(kcs_all[r::4, g, :, :],
                                     part[32 * g:32 * g + 32, :].bitcast(F32).rearrange("p (b t) -> p b t", b=B)
                                     ).then_inc(kc_stacked, 16)

            def load_ffn_weights():
                for dst, k in ((w13[:, 0, 0:E * HID], "w1T"), (w13[:, 1, 0:E * HID], "w3T"),
                               (w13[:, 0, E * HID:(E + 1) * HID], "sw1T"), (w13[:, 1, E * HID:(E + 1) * HID], "sw3T"),
                               (w2[:, 0:E // 2, :], "w2T"), (gw[:], "gwT"), (sel_f[:], "sel")):
                    sp.dma_start(dst, a[k]).then_inc(w13_in, 16)
                sp.wait_ge(ffn_consts, 2)
                sp.dma_start(w2[0:HID, E // 2, :], a["sw2T"]).then_inc(w13_in, 16)

            def slot(t):
                if has_prep(t.n):
                    st = stack[(t.n // 2 + 1) % 2]
                    if t.n == -2:
                        sp.wait_ge(zeros_set, 1)
                        sp.wait_ge(stack_set[0], 2)
                    if t.n == 0:
                        sp.wait_ge(stack_set[1], 2)
                    wait(sp, sc_filled, t, lambda n: 16 * attends(n - 1))
                    for g in range(G):
                        sp.dma_start(st[3::16, 1:3, g, :].bitcast(F32),
                                     zero8[:, :].rearrange("p (x t) -> p x t", x=2)).then_inc(stacked, 16)
                    for r, dst, src, sem, made in (
                            (0, slice(0, 1), slice(3, 4), hi_made, lambda n: 3 * preps(n - 1) + 2),
                            (0, slice(1, 3), slice(1, 3), hi_made, lambda n: 3 * preps(n - 1) + 3),
                            (1, slice(0, 3), slice(0, 3), sh_emptied[1], emptied("qc")),
                            (2, slice(0, 3), slice(3, 6), sh_emptied[1], emptied("qc"))):
                        if r < 2:
                            wait(sp, sem, t, made)
                        for g in range(G):
                            rows = slice(32 * g, 32 * g + 32)
                            sp.dma_start(st[r::4, dst, g, :].bitcast(F32),
                                         parts[rows, src, :].bitcast(F32)).then_inc(stacked, 16)
                if t.n == -2:
                    stack_context()
                if has_max(t.n):
                    m = t.n + 1
                    st = stack[(m // 2) % 2]
                    wait(sp, sh_emptied[1], t, emptied("mT"))
                    for g in range(G):
                        sp.dma_start(st[3::16, 1:3, g, T * (m % 2):T * (m % 2) + T].bitcast(F32),
                                     mT[8 * g:8 * g + 8, :, :]).then_inc(m_stacked, 16)
                if t.n == 0:
                    load_ffn_weights()

            attention_slots(sp, slot)
            o_t = out.rearrange("(n p) c -> p n c", p=128)

            def ffn_slot(t):
                if 1 <= t.n <= 8:
                    wait(sp, x3_made, t, ffn_downs)
                    tiles = ds(t.at(lambda j: 4 * (j - 1)), 4)
                    sp.dma_start(o_t[:, tiles, :], xs[:, tiles, :]).then_inc(out_done, 16)

            ffn_slots(sp, ffn_slot)
            sp.wait_ge(out_done, 16 * NF)

        @block.gpsimd
        def _(pool):
            nc.gpsimd.memset(zero8[:], 0.0).then_inc(zeros_set, 1)
            nc.gpsimd.memset(half[:], -0.5).then_inc(half_set, 1)
            nc.gpsimd.memset(stack[0][:, 0].bitcast(F32), 1.0).then_inc(stack_set[0], 1)

            def tiles_rstd(lo, hi, nth):
                t = slice(lo, hi)
                nc.gpsimd.tensor_tensor(rs0[:, t], vare[:, t], half[:, t], ALU.pow).then_inc(rstd_made, 1)
                pool.wait_ge(rstd_made, 5 * nth + 1)
                nc.gpsimd.tensor_tensor(rs1[:, t], rs0[:, t], rs0[:, t], ALU.mult).then_inc(rstd_made, 1)
                pool.wait_ge(rstd_made, 5 * nth + 2)
                nc.gpsimd.tensor_tensor(rs1[:, t], rs1[:, t], vare[:, t], ALU.mult).then_inc(rstd_made, 1)
                pool.wait_ge(rstd_made, 5 * nth + 3)
                nc.gpsimd.tensor_scalar(rs1[:, t], rs1[:, t], -0.5, 1.5, ALU.mult, ALU.add).then_inc(rstd_made, 1)
                pool.wait_ge(rstd_made, 5 * nth + 4)
                nc.gpsimd.tensor_tensor(rstd[:, t], rs1[:, t], rs0[:, t], ALU.mult).then_inc(rstd_made, 1)

            pool.wait_ge(half_set, 1)
            pool.wait_ge(aggregated, 1)
            tiles_rstd(*SECTIONS[0], 0)
            nc.gpsimd.memset(kcs_all[:], 1.0).then_inc(kcs_set, 1)
            nc.gpsimd.memset(vcz[:], 0.0).then_inc(pool_consts, 1)
            nc.gpsimd.memset(vz[:], 0.0).then_inc(pool_consts, 1)
            pool.wait_ge(pool_consts, 2)
            for z in range(2):
                for kt in range(2):
                    for ab in range(2):
                        nc.gpsimd.memset(vz[:, z, kt, ab, 64:648].rearrange("p (h x) -> p h x", x=73)[:, :, 0:1],
                                         1.0).then_inc(pool_consts, 1)

            def context_keys(t):
                if t.n == -2:
                    pool.wait_ge(kc_stacked, 16 * 12)
                    pool.wait_ge(fixed_in, 16)
                wait(pool, sc_filled, t, lambda n: 16 * attends(n - 2))
                src = kcs_all[:, :, ds(t.at(lambda n: n + 2), 1), :].rearrange("p g b t -> p g (b t)")
                nc.gpsimd.tensor_tensor(
                    kcs[:, (t.n + 2) % 4, :, :, :],
                    src.unsqueeze(2).broadcast_to([128, G, 2, TC]),
                    par_mask[:, :].unsqueeze(1).unsqueeze(3).broadcast_to([128, G, 2, TC]),
                    ALU.mult).then_inc(kcs_made, 1)

            def values(t):
                if t.n == -1:
                    pool.wait_ge(vc_made, 8)
                    pool.wait_ge(pool_consts, 10)
                wait(pool, pv_done, t, lambda n: 8 * attends(n - 1))
                z = (t.n + 1) % 2
                nc.gpsimd.tensor_tensor(
                    vcz[:, z, :, 0:352].rearrange("p a (j x) -> p a j x", x=88)[:, :, :, 0:16],
                    vc_all[:, ds(t.at(lambda n: n + 1), 1), :].rearrange("p b (a j x) -> p (b a) j x", a=2, j=4),
                    half_mask[:].unsqueeze(1).unsqueeze(1).broadcast_to([128, 2, 4, 2 * D]),
                    ALU.mult).then_inc(vz_made, 1)
                wait(pool, sh_emptied[0], t, lambda n: emptied("v")(2 * ((n + 1) // 2) - 2))
                for ab in range(2):
                    nc.gpsimd.tensor_tensor(
                        vz[:, z, :, ab, 0:640].rearrange("p k (h x) -> p k h x", x=80)[:, :, :, 0:D],
                        vst[:, ((t.n + 1) // 2) % 2, 2 * z:2 * z + 2, 64 * ab:64 * ab + 64].rearrange(
                            "p k (h d) -> p k h d", d=D),
                        bv_b[:, 64 * ab:64 * ab + 64].rearrange("p (h d) -> p h d", d=D).unsqueeze(1)
                        .broadcast_to([128, 2, 8, D]), ALU.add).then_inc(vz_made, 1)

            def causal(t, c, kind):
                wait(pool, exp_done, t, lambda n: 16 * attends(n - 1) + c + 1)
                pool.sem_inc(mask_turns, 1)
                nh = 2 if kind == "k0" else 4
                blk = probs[:, c % RING, :].rearrange("p (h q) -> p h q", h=nh)[:, :, 0:128]
                nc.gpsimd.affine_select(out=blk, in_=blk, pattern=[[0, nh], [1, 128]],
                                        compare_op=ALU.is_ge, fill=0.0, base=0,
                                        channel_multiplier=-1).then_inc(masked, 1)

            def chunk_rstd(t):
                wait(pool, stats2, t, lambda j: 3 * ffn_stats(j))
                wait(pool, xn2_made, t, lambda j: ffn_preps(j))
                steps = ((rt0, ve2, half2, ALU.pow), (rt1, rt0, rt0, ALU.mult), (rt1, rt1, ve2, ALU.mult))
                for k, (dst, x, y_, op) in enumerate(steps):
                    if k:
                        wait(pool, rstd2_steps, t, lambda j: 5 * ffn_stats(j - 1) + k)
                    nc.gpsimd.tensor_tensor(dst[:], x[:], y_[:], op).then_inc(rstd2_steps, 1)
                wait(pool, rstd2_steps, t, lambda j: 5 * ffn_stats(j - 1) + 3)
                pool.sem_inc(mask_turns, 1)
                nc.gpsimd.tensor_scalar(rt1[:], rt1[:], -0.5, 1.5, ALU.mult, ALU.add).then_inc(rstd2_steps, 1)
                wait(pool, rstd2_steps, t, lambda j: 5 * ffn_stats(j - 1) + 4)
                nc.gpsimd.tensor_tensor(rstd2[:], rt1[:], rt0[:], ALU.mult).then_inc(rstd2_steps, 1)

            def slot(t):
                if t.n == FIRST_PREP:
                    pool.wait_ge(sc_filled, front_free)
                    nc.gpsimd.memset(half2[:], -0.5).then_inc(ffn_consts, 1)
                    nc.gpsimd.memset(pr[:, :, E:E + 4], -1.0).then_inc(ffn_consts, 1)
                    nc.gpsimd.memset(picks[:, :, 4:8], -1.0).then_inc(ffn_consts, 1)
                for c in range(13):
                    if t.n == FIRST_PREP and c == 1:
                        pool.wait_ge(ffn_consts, 5)
                        chunk_rstd(Slot(-2))
                    if has_attend(t.n) and c < 12:
                        causal(t, c, score_chunks()[c][0])
                    if has_out(t.n) and c == 2:
                        tiles = ds(t.at(lambda n: 2 * (n - 1)), 2)
                        if t.n == 1:
                            pool.wait_ge(pool_consts, 11)
                        wait(pool, xn_made, t, lambda n: preps(n - 1))
                        nc.gpsimd.tensor_tensor(xs[:, tiles, :], xs[:, tiles, :],
                                                bpg[:].unsqueeze(1).broadcast_to([128, 2, C]),
                                                ALU.add).then_inc(xb_made, 1)
                    if has_out(t.n) and c == 6:
                        wait(pool, sh_emptied[1], t, emptied("o0"))
                        wait(pool, sh_emptied[0], t, emptied("o1"))
                        if t.n >= 2:
                            wait(pool, sh_filled, t, lambda n: filled("yT")(n - 1))
                        nc.gpsimd.tensor_tensor(y[:], normed[:, :, 0, :], normed[:, :, 1, :],
                                                ALU.add).then_inc(y_made, 1)
                    if -2 <= t.n <= 13 and c == 8:
                        context_keys(t)
                    if -1 <= t.n <= 14 and c == 12:
                        values(t)
                if t.n == -2:
                    nc.gpsimd.memset(stack[1][:, 0].bitcast(F32), 1.0).then_inc(stack_set[1], 1)
                    nc.gpsimd.memset(stack[1][:, 1:3].bitcast(F32), 0.0).then_inc(stack_set[1], 1)
                    nc.gpsimd.memset(w13[:, :, (E + 1) * HID:FK * 128], 0.0).then_inc(ffn_consts, 1)
                    nc.gpsimd.memset(w2[:, E // 2, :], 0.0).then_inc(ffn_consts, 1)
                if t.n == -1:
                    pool.wait_ge(tg_made, 1)
                    nc.gpsimd.tensor_scalar(bpg[:], bp_b[:], tg[:, 0:1], None, ALU.mult).then_inc(pool_consts, 1)
                if t.n == 0:
                    pool.wait_ge(aggregated, len(SECTIONS))
                    tiles_rstd(SECTIONS[1][0], NT, 1)
                if t.n == FIRST_PREP:
                    chunk_rstd(Slot(-1))

            attention_slots(pool, slot)

            def ffn_slot(t):
                if t.n <= 5:
                    chunk_rstd(t)

            ffn_slots(pool, ffn_slot)

        @block.scalar
        def _(act):
            act.dma_start(fixed[:], a["fixed"]).then_inc(fixed_in, 16)
            act.dma_start(gates[:], a["gates"].rearrange("(o c) -> o c", o=1).broadcast_to([128, 2])
                          ).then_inc(gates_in, 16)
            act.dma_start(w_all[:].rearrange("p k c -> p (k c)"), a["w_all"]).then_inc(weights_in, 16)
            act.dma_start(bcol[:], a["bcol"]).then_inc(weights_in, 16)
            act.dma_start(wc_all[:].rearrange("p k c -> p (k c)"), a["wc_all"]).then_inc(ctx_in, 16)
            for e in range(2):
                act.dma_start(cT2[:, :, e, :], a["ctxT"].rearrange("p (b t) -> p b t", b=B)).then_inc(ctx_in, 16)
            act.dma_start(qmaskf[:].rearrange("p h k -> p (h k)"), a["qmask"]).then_inc(rest_in, 16)
            act.dma_start(brow[:].rearrange("p k c -> p (k c)"),
                          a["brow"].rearrange("(o c) -> o c", o=1).broadcast_to([128, 3 * C])).then_inc(rest_in, 16)
            act.wait_ge(gates_in, 16)
            nc.scalar.activation(tg[:], gates[:], ACT.Tanh).then_inc(tg_made, 1)
            act.wait_ge(weights_in, n_weights)

            def context_keys():
                for j in range(2):
                    act.wait_ge(kc_filled, j + 1)
                    nc.scalar.activation(kc_hi[:, 512 * j:512 * j + 512], psc[j][:, :], ACT.Identity,
                                         bias=bcol[:, 3:4]).then_inc(kc_hi_made, 1)

            def hi(t, kind, bank, dst, col):
                wait(act, sh_filled, t, filled(kind))
                nc.scalar.activation(parts[:, dst, :], psh[bank][:, :], ACT.Identity,
                                     bias=bcol[:, col:col + 1]).then_inc(hi_made, 1)

            def split_ffn_weights():
                act.wait_ge(w13_in, n_w13)
                act.wait_ge(ffn_consts, 2)
                act.wait_ge(sc_filled, 16 * attends(13))
                for k in range(2):
                    nc.scalar.activation(w13_parts[:, 0, k, :], w13[:, k, :], ACT.Copy).then_inc(w13_hi_made, 1)
                nc.scalar.activation(gw_parts[:, 0, :], gw[:], ACT.Copy).then_inc(w13_hi_made, 1)
                nc.scalar.activation(sel[:].rearrange("p k c -> p (k c)"), sel_f[:],
                                     ACT.Copy).then_inc(w13_hi_made, 1)

            def ffn_prepare(t, k):
                z, pT2 = (t.n + 1) % 2, transposed_bank(t.n)
                if k == 1:
                    wait(act, xT2_filled, t, ffn_preps)
                    if t.n >= 1:
                        wait(act, h_filled, t, lambda j: FK * ffn_mains(j - 1))
                    nc.scalar.activation(x_hi[:, z, :], pT2[:, :], ACT.Copy).then_inc(x_hi_made, 1)
                if k == 4:
                    wait(act, gate_steps, t, lambda j: GATE_STEPS * ffn_preps(j - 1) + 2)
                    nc.scalar.activation(expd[:], shifted[:], ACT.Exp).then_inc(exp2_made, 1)

            def silu_tile(t, k):
                q = FK * (t.n % 2) + k
                wait(act, h_filled, t, lambda j: FK * ffn_mains(j - 1) + k + 1)
                wait(act, gated_made, t, lambda j: FK * ffn_mains(j - 1) + k - 1)
                nc.scalar.activation(silu[:, q % 2, :], ph1[q % 2][:, :], ACT.Silu).then_inc(silu_made, 1)
                if k == 0:
                    wait(act, combT_filled, t, lambda j: j + 1)
                    nc.scalar.activation(combT[:, t.n % 2, :], transposed_bank(t.n - 1)[0:2 * E, :],
                                         ACT.Copy).then_inc(combT_made, 1)

            def slot(t):
                if has_prep(t.n):
                    wait(act, sh_filled, t, filled("xT"))
                    nc.scalar.activation(xnT[:], psh[0][:, :], ACT.Copy).then_inc(sh_emptied[0], 1)
                for c in range(16):
                    if has_out(t.n) and c in (0, 3):
                        wait(act, pv_done, t, lambda n: 8 * attends(n - 1) - (4 if c == 0 else 0))
                        if t.n >= 2:
                            wait(act, sh_filled, t, lambda n: filled("o1")(n - 1))
                        nc.scalar.activation(pcopy[:, c // 3, :], (pself, pcross)[c // 3][0:VR, :],
                                             ACT.Copy).then_inc(copied, 1)
                    if has_attend(t.n):
                        wait(act, sc_filled, t, lambda n: 16 * attends(n - 1) + c + 1)
                        wait(act, pv_done, t, lambda n: 8 * attends(n - 1) + ((c - 8) // 3 + 1 if c >= 8 else
                                                                              ((c + 8) // 3 + 1 if c < 4 else c + 1) - 8))
                        nc.scalar.activation(probs[:, c % RING, :], psc[c % 2][:, :], ACT.Exp,
                                             scale=SCALE).then_inc(exp_done, 1)
                    if has_prep(t.n) and c in (1, 2, 3):
                        if c == 1:
                            wait(act, stacked, t, lambda n: 16 * PREP_DMAS * preps(n - 1))
                        kind, bank, dst, col = (("q", 1, 1, 0), ("k", 0, 3, 1), ("qc", 1, 2, 2))[c - 1]
                        hi(t, kind, bank, dst, col)
                    if t.n == -2 and c == 3:
                        context_keys()
                    if has_out(t.n) and c == 8:
                        wait(act, sh_filled, t, filled("yT"))
                        nc.scalar.activation(yT[:].rearrange("p a b -> p (a b)"), psh[1][:, 0:256],
                                             ACT.Copy).then_inc(sh_emptied[1], 1)
                    if has_max(t.n) and c == 12:
                        wait(act, sh_filled, t, filled("mT"))
                        wait(act, m_stacked, t, lambda n: 16 * MAX_DMAS * maxes(n - 1))
                        nc.scalar.activation(mT[:].rearrange("p a b -> p (a b)"), psh[1][0:32, :],
                                             ACT.Copy).then_inc(sh_emptied[1], 1)
                    if t.n == 16 and c in EARLY_AT:
                        silu_tile(Slot(0), EARLY_AT.index(c))
                    if t.n == FIRST_PREP - 1 and c == 14:
                        split_ffn_weights()
                    if t.n == FIRST_PREP and c in STAGE_AT:
                        ffn_prepare(Slot(-1), STAGE_AT.index(c))

            attention_slots(act, slot)
            act.wait_ge(sh_emptied[0], attention_done)

            def ffn_slot(t):
                for k in range(FK):
                    if 0 <= t.n <= 7:
                        if t.n > 0 or k >= len(EARLY_AT):
                            silu_tile(t, k)
                    if t.n <= 6:
                        ffn_prepare(t, k)

            ffn_slots(act, ffn_slot)

        @block.vector
        def _(dve):
            nc.vector.memset(stack[0][:, 1:3].bitcast(F32), 0.0).then_inc(stack_set[0], 1)

            def statistics(section):
                lo, hi = SECTIONS[section]
                for k in range(lo, hi):
                    for j, (first, _) in enumerate(LOADS):
                        if k == first:
                            dve.wait_ge(x_in[j], 16)
                    nc.vector.bn_stats(stat[:, k, :], xs[:, k, :]).then_inc(stats_made, 1)
                for k in range(lo, hi):
                    dve.wait_ge(stats_made, k + 1)
                    i = nc.vector.bn_aggr(mv[:, k, :], stat[:, k, :])
                i.then_inc(mv_made, 1)
                dve.wait_ge(mv_made, section + 1)
                nc.vector.tensor_scalar(vare[:, lo:hi], mv[:, lo:hi, 1], EP, None, ALU.add).then_inc(aggregated, 1)

            statistics(0)
            dve.wait_ge(rstd_made, 5)

            def context_keys():
                for j in range(2):
                    dve.wait_ge(kc_hi_made, j + 1)
                    nc.vector.scalar_tensor_tensor(
                        kc_lo[:, 512 * j:512 * j + 512], psc[j][:, :], bcol[:, 3:4],
                        kc_hi[:, 512 * j:512 * j + 512].bitcast(F32), ALU.add, ALU.subtract).then_inc(kc_lo_made, 1)

            def context_values():
                dve.wait_ge(rest_in, n_rest)
                dve.wait_ge(fixed_in, 16)
                nc.vector.tensor_copy(identb[:], ident[:]).then_inc(masks_made, 1)
                nc.vector.tensor_copy(qmask[:].rearrange("p h k -> p (h k)"),
                                      qmaskf[:].rearrange("p h k -> p (h k)")).then_inc(masks_made, 1)
                for q in range(4):
                    dve.wait_ge(vc_filled, q + 1)
                    src = (psc[0], psc[1], pself, pcross)[q]
                    nc.vector.tensor_tensor(vc_all[:, 4 * q:4 * q + 4, :],
                                            src[:, :].rearrange("p (b c) -> p b c", b=4),
                                            bcv_b[:].unsqueeze(1).broadcast_to([128, 4, C]),
                                            ALU.add).then_inc(vc_made, 1)
                dve.wait_ge(pool_consts, 2)
                for e in range(2):
                    for z in range(2):
                        nc.vector.memset(vcz[64 * e:64 * e + 64, z, :, 64 + e:360 + e].rearrange(
                            "p a (j x) -> p a j x", x=74)[:, :, :, 0:1], 1.0).then_inc(vc_made, 1)

            def make_xn(t):
                if t.n > -3:
                    wait(dve, sh_filled, t, lambda n: filled("xT")(n - 1))
                for k in range(4):
                    tile = t.at(lambda n: 2 * (n + 3) + k)
                    mean = mv[:, ds(tile, 1), 0:1].rearrange("p a b -> p (a b)")
                    i = nc.vector.tensor_scalar(xn[:, k, :], xs[:, ds(tile, 1), :].rearrange("p a c -> p (a c)"),
                                                mean, rstd[:, ds(tile, 1)],
                                                ALU.subtract, ALU.mult)
                i.then_inc(xn_made, 1)

            make_xn(Slot(-3))

            def lo(t, kind, bank, hi_part, lo_part, col, nth):
                wait(dve, hi_made, t, lambda n: 3 * preps(n - 1) + nth + 1)
                nc.vector.scalar_tensor_tensor(
                    parts[:, lo_part, :], psh[bank][:, :], bcol[:, col:col + 1],
                    parts[:, hi_part, :].bitcast(F32), ALU.add, ALU.subtract).then_inc(sh_emptied[bank], 1)

            def bc4(x, n):
                return x[:].unsqueeze(2).broadcast_to([128, 4, n])

            def split_ffn_weights(k):
                dve.wait_ge(w13_hi_made, k + 1)
                if k < 2:
                    nc.vector.tensor_tensor(w13_parts[:, 1, k, :], w13[:, k, :], w13_parts[:, 0, k, :].bitcast(F32),
                                            ALU.subtract).then_inc(w13_lo_made, 1)
                else:
                    nc.vector.tensor_tensor(gw_parts[:, 1, :], gw[:], gw_parts[:, 0, :].bitcast(F32),
                                            ALU.subtract).then_inc(w13_lo_made, 1)

            def chunk_tile(t, k, count=1):
                return ds(t.at(lambda j: 4 * (j + 1) + k), count)

            def chunk_statistics(t):
                for x in range(4):
                    ins = nc.vector.bn_stats(stat2[:, x, :], xs[:, chunk_tile(t, x + 4), :].rearrange(
                        "p a c -> p (a c)"))
                ins.then_inc(stats2, 1)
                wait(dve, stats2, t, lambda j: 3 * ffn_stats(j) - 2)
                dve.sem_inc(dve_turns, 1)
                for x in range(4):
                    ins = nc.vector.bn_aggr(mv2[:, x, :], stat2[:, x, :])
                ins.then_inc(stats2, 1)
                wait(dve, stats2, t, lambda j: 3 * ffn_stats(j) - 1)
                nc.vector.tensor_scalar(ve2[:], mv2[:, :, 1], EP, None, ALU.add).then_inc(stats2, 1)

            def ffn_prepare(t, k):
                z, pT2 = (t.n + 1) % 2, transposed_bank(t.n)

                def gate_step(nth, ins):
                    ins.then_inc(gate_steps, 1)
                    wait(dve, gate_steps, t, lambda j: GATE_STEPS * ffn_preps(j - 1) + nth)

                if k == 0:
                    wait(dve, rstd2_steps, t, lambda j: 5 * ffn_preps(j))
                    wait(dve, xT2_filled, t, lambda j: ffn_preps(j - 1))
                    for x in range(4):
                        ins = nc.vector.tensor_scalar(xn2[:, x, :], xs[:, chunk_tile(t, x), :].rearrange(
                            "p a c -> p (a c)"), mv2[:, x, 0:1], rstd2[:, x:x + 1], ALU.subtract, ALU.mult)
                    ins.then_inc(xn2_made, 1)
                if k == 1:
                    wait(dve, x_hi_made, t, ffn_preps)
                    nc.vector.tensor_tensor(x_lo[:, z, :], pT2[:, :], x_hi[:, z, :].bitcast(F32),
                                            ALU.subtract).then_inc(x_lo_made, 1)
                if k == 1 and t.n <= 5:
                    chunk_statistics(t)
                if k == 3:
                    wait(dve, gate_filled, t, ffn_preps)
                    logits = pT2[:, 0:4 * E].rearrange("p (k e) -> p k e", e=E)
                    gate_step(1, nc.vector.tensor_reduce(nmx[:], logits, axis=AX_X, op=ALU.max, negate=True))
                    gate_step(2, nc.vector.tensor_tensor(shifted[:], logits, bc4(nmx, E), ALU.add))
                if k == 4:
                    wait(dve, exp2_made, t, ffn_preps)
                    if t.n == -1:
                        dve.wait_ge(ffn_consts, 5)
                    gate_step(3, nc.vector.tensor_reduce(esum[:], expd[:], axis=AX_X, op=ALU.add))
                    gate_step(4, nc.vector.reciprocal(erec[:], esum[:]))
                    gate_step(5, nc.vector.tensor_tensor(pr[:, :, 0:E], expd[:], bc4(erec, E), ALU.mult))
                if k == 5:
                    dve.sem_inc(dve_turns, 1)
                    for x in range(4):
                        ins = nc.vector.max(top8[:, x, :], pr[:, x, 0:E])
                    gate_step(6, ins)
                    gate_step(7, nc.vector.tensor_copy(picks[:, :, 0:TOPK], top8[:, :, 0:TOPK]))
                    dve.sem_inc(dve_turns, 1)
                    for x in range(4):
                        ins = nc.vector.match_replace(marked[:, x, :], picks[:, x, :], pr[:, x, :], -2.0)
                    gate_step(8, ins)
                if k == 6:
                    gate_step(9, nc.vector.scalar_tensor_tensor(chosen[:], marked[:, :, 0:E], -1.5,
                                                                pr[:, :, 0:E], ALU.is_lt, ALU.mult))
                    gate_step(10, nc.vector.tensor_reduce(wsum[:], chosen[:], axis=AX_X, op=ALU.add))
                    gate_step(11, nc.vector.reciprocal(wrec[:], wsum[:]))
                    gate_step(12, nc.vector.tensor_tensor(comb[:], chosen[:], bc4(wrec, E), ALU.mult))
                if k == 7:
                    wait(dve, combT_filled, t, lambda j: ffn_preps(j - 1))
                    gate_step(13, nc.vector.tensor_copy(comb_parts[:, :, 0, :], comb[:]))
                    gate_step(14, nc.vector.tensor_tensor(comb_parts[:, :, 1, :], comb[:],
                                                          comb_parts[:, :, 0, :].bitcast(F32), ALU.subtract))

            def slot(t):
                for c, chunks in enumerate(max_steps(t.n)):
                    if has_prep(t.n) and c in (1, 2, 3):
                        lo(t, *(("q", 1, 1, 4, 0), ("k", 0, 3, 0, 1), ("qc", 1, 2, 5, 2))[c - 1], c - 1)
                    for k, (kind, i, j) in chunks:
                        if k == 0:
                            wait(dve, mparts_made, t, lambda n: 2 * maxes(n - 1))
                        wait(dve, max_filled, t, lambda n: 16 * maxes(n - 1) + k + 1)
                        src = max_banks(t)[k % len(max_banks(t))][:, :]
                        if kind == "q0":
                            dst = negmax[:, 0, 0, :].rearrange("p (g i) -> p g i", g=G)[:, :, i]
                            src = src.rearrange("p (g k) -> p g k", g=4)
                        elif kind == "q1":
                            dst = negmax[:, 0, 1, :].rearrange("p (g i) -> p g i", g=G)[:, 2 * j:2 * j + 2, i]
                            src = src.rearrange("p (g k) -> p g k", g=2)
                        else:
                            dst = negmax[:, 1, j, :].rearrange("p (g i) -> p g i", g=G)[:, :, 2 * i:2 * i + 2]
                            src = src.rearrange("p (g e k) -> p g e k", g=G, e=2)
                        nc.vector.tensor_reduce(dst, src, axis=AX_X, op=ALU.max, negate=True).then_inc(max_read, 1)
                    if has_prep(t.n) and c == 4:
                        wait(dve, sh_filled, t, filled("v"))
                        if t.n >= 0:
                            wait(dve, vz_made, t, lambda n: 3 * attends(n))
                        nc.vector.tensor_copy(vst[:, (t.n // 2 + 1) % 2, :, :].rearrange("p k c -> p (k c)"),
                                              psh[0][:, :]).then_inc(sh_emptied[0], 1)
                    if has_out(t.n) and c == 5:
                        for qt, kind in ((0, "o0"), (1, "o1")):
                            wait(dve, sh_filled, t, filled(kind))
                            o = psh[BANK[kind]][:, 0:4 * VR].rearrange("p (x r) -> p x r", r=VR)
                            rd = rden[:, qt, :].rearrange("p (x h) -> p x h", h=8)
                            nc.vector.reciprocal(rd, o[:, :, 64:VR]).then_inc(recips, 1)
                            wait(dve, recips, t, lambda n: 2 * outs(n) - 1 + qt)
                            wait(dve, y_made, t, lambda n: outs(n - 1))
                            nc.vector.tensor_tensor(
                                normed[:, qt, :, :].rearrange("p x (a h d) -> p (x a) h d", a=2, d=D),
                                o[:, :, 0:64].rearrange("p x (h d) -> p x h d", d=D),
                                rd.unsqueeze(3).broadcast_to([128, 4, 8, D]),
                                ALU.mult).then_inc(sh_emptied[BANK[kind]], 1)
                    if has_out(t.n) and c == 10:
                        wait(dve, sh_filled, t, filled("proj"))
                        wait(dve, xb_made, t, lambda n: outs(n))
                        tiles = ds(t.at(lambda n: 2 * (n - 1)), 2)
                        nc.vector.scalar_tensor_tensor(
                            xs[:, tiles, :].rearrange("p a c -> p (a c)"), psh[0][:, 0:256], tg[:, 0:1],
                            xs[:, tiles, :].rearrange("p a c -> p (a c)"), ALU.mult,
                            ALU.add).then_inc(sh_emptied[0], 1)
                    if has_max(t.n) and c == 10:
                        wait(dve, max_read, t, lambda n: 16 * maxes(n))
                        if t.n > -1:
                            wait(dve, sh_filled, t, lambda n: filled("mT")(n - 1))
                        nm = negmax[:].rearrange("p x q h -> p (x q h)")
                        mp = mparts[:].rearrange("p x q h e -> p (x q h) e")
                        nc.vector.tensor_copy(mp[:, :, 0], nm).then_inc(mparts_made, 1)
                        wait(dve, mparts_made, t, lambda n: 2 * maxes(n) - 1)
                        nc.vector.tensor_tensor(mp[:, :, 1], nm, mp[:, :, 0].bitcast(F32),
                                                ALU.subtract).then_inc(mparts_made, 1)
                    if t.n == -2 and c == 4:
                        context_keys()
                        context_values()
                    if t.n == 0 and c >= 13:
                        statistics(c - 12)
                    if has_prep(t.n + 1) and c == 12:
                        if t.n == 1:
                            dve.wait_ge(rstd_made, 10)
                        make_xn(t)
                    if t.n == FIRST_PREP:
                        if c == 0:
                            dve.wait_ge(sc_filled, front_free)
                            chunk_statistics(Slot(-2))
                        if c < 3:
                            split_ffn_weights(c)
                        if c in STAGE_AT:
                            ffn_prepare(Slot(-1), STAGE_AT.index(c))

            attention_slots(dve, slot)
            dve.wait_ge(sh_emptied[0], attention_done)

            def ffn_slot(t):
                for k in range(FK):
                    if k == FK - 1 and t.n >= 1:
                        wait(dve, down_filled, t, ffn_downs)
                        tiles = ds(t.at(lambda j: 4 * (j - 1)), 4)
                        x3 = xs[:, tiles, :].rearrange("p a c -> p (a c)")
                        nc.vector.scalar_tensor_tensor(x3, py[:, :], tg[:, 1:2], x3, ALU.mult,
                                                       ALU.add).then_inc(x3_made, 1)
                    if t.n <= 7:
                        z, q = t.n % 2, FK * (t.n % 2) + k
                        wait(dve, silu_made, t, lambda j: FK * ffn_mains(j - 1) + k + 1)
                        if k == 0:
                            wait(dve, down_filled, t, lambda j: ffn_mains(j - 2))
                        if k >= 2 or t.n > 0:
                            wait(dve, hidden_made, t, lambda j: (FK - 1) * ffn_mains(j - 1) + min(max(k - 1, 0), 8))
                        dst = gated[:, q % 2, :] if k < FK - 1 else hidden[:, z, k, :]
                        nc.vector.tensor_tensor(dst, silu[:, q % 2, :], ph3[q % 2][:, :],
                                                ALU.mult).then_inc(gated_made, 1)
                        if k < FK - 1:
                            wait(dve, cb_filled, t, lambda j: (FK - 1) * ffn_mains(j - 1) + k + 1)
                            wait(dve, gated_made, t, lambda j: FK * ffn_mains(j - 1) + k + 1)
                            nc.vector.tensor_tensor(hidden[:, z, k, :], gated[:, q % 2, :], pcb[k % 2][:, :],
                                                    ALU.mult).then_inc(hidden_made, 1)
                    if t.n <= 6:
                        ffn_prepare(t, k)

            ffn_slots(dve, ffn_slot)

        @block.tensor
        def _(pe):
            def context_keys():
                pe.wait_ge(ctx_in, n_ctx)
                for j in range(2):
                    nc.tensor.matmul(psc[j][:, :], wck[:], cT2[:, 8 * j:8 * j + 8, 0, :],
                                     start=True, stop=True).then_inc(kc_filled, 1)

            def context_values():
                pe.wait_ge(kc_lo_made, 2)
                for q in range(4):
                    dst = (psc[0], psc[1], pself, pcross)[q]
                    for b in range(4):
                        i = nc.tensor.matmul(dst[:, C * b:C * b + C],
                                             cT2[:, 4 * q + b, :, :].rearrange("p e t -> p (e t)"),
                                             wcv[:], start=True, stop=True)
                    i.then_inc(vc_filled, 1)

            def wait_bank(t, kind):
                wait(pe, sh_emptied[BANK[kind]], t, lambda n: emptied(kind)(n) - 1)

            def project(t, kind, w):
                wait_bank(t, kind)
                if kind == "q":
                    wait(pe, sh_emptied[0], t, emptied("xT"))
                nc.tensor.matmul(psh[BANK[kind]][:, :], w[:], xnT[:], start=True, stop=True).then_inc(sh_filled, 1)

            def max_chunk(t, k, kind, i, j):
                m = t.n + 1
                st = stack[(m // 2) % 2]
                kt, qt, qct = st[:, 0], st[:, 1], st[:, 2]
                b = T * (m % 2)
                bank = max_banks(t)[k % len(max_banks(t))]
                if t.n == -1 and k == 2:
                    pe.wait_ge(vc_made, 2)
                if k == 0:
                    wait(pe, stacked, t, lambda n: 16 * PREP_DMAS * ((n + 1) // 2 + 1))
                    if t.n == -1:
                        pe.wait_ge(masks_made, 2)
                if k == 12:
                    wait(pe, kcs_made, t, lambda n: n + 2)
                wait(pe, max_read, t, lambda n: 16 * maxes(n - 1) + k + 1 - len(max_banks(t)))
                if kind == "c":
                    rows = slice(64 * i, 64 * i + 64)
                    for g in range(G):
                        last = nc.tensor.matmul(bank[:, 128 * g:128 * g + 128],
                                                qct[rows, g, b + 128 * j:b + 128 * j + 128],
                                                kcs[rows, m % 4, g, :, :].rearrange("p e t -> p (e t)"),
                                                start=(g == 0), stop=(g == G - 1))
                else:
                    rows = slice(32 * i, 32 * i + 32)
                    heads = range(4) if kind == "q0" else range(2 * j, 2 * j + 2)
                    w = 128 if kind == "q0" else 256
                    q0 = b + (0 if kind == "q0" else 128)
                    for x, g in enumerate(heads):
                        nc.tensor.matmul(bank[:, w * x:w * x + w], qt[rows, g, q0:q0 + 128], kt[rows, g, b:b + w],
                                         start=(x == 0), stop=False)
                    nh = len(heads)
                    last = nc.tensor.matmul(bank[:, :].rearrange("p (h k) -> p h k", h=nh)[:, :, w - 128:w],
                                            identb[:], qmask[:, 0:nh, :], start=False, stop=True)
                last.then_inc(max_filled, 1)

            def score_chunk(t, c, kind, i, j):
                st = stack[(t.n // 2) % 2]
                kt, qt, qct = st[:, 0], st[:, 1], st[:, 2]
                b = T * (t.n % 2)
                bank = psc[c % 2]
                wait(pe, exp_done, t, lambda n: 16 * attends(n - 1) + c - 1)
                if c == 0:
                    wait(pe, m_stacked, t, lambda n: 16 * MAX_DMAS * (n + 1))
                if kind == "k1":
                    for g in range(G):
                        last = nc.tensor.matmul(bank[:, 128 * g:128 * g + 128], kt[32 * i:32 * i + 32, g, b + 128:b + 256],
                                                qt[32 * i:32 * i + 32, g, b + 128:b + 256], start=True, stop=True)
                else:
                    for x, g in enumerate((2 * j, 2 * j + 1)):
                        if kind == "k0":
                            rows = slice(32 * i, 32 * i + 32)
                            keys, q = kt[rows, g, b:b + 128], qt[rows, g, b:b + 256]
                        else:
                            rows = slice(64 * i, 64 * i + 64)
                            keys = kcs[rows, t.n % 4, g, :, :].rearrange("p e t -> p (e t)")
                            q = qct[rows, g, b:b + 256]
                        last = nc.tensor.matmul(bank[:, 256 * x:256 * x + 256], keys, q, start=True, stop=True)
                last.then_inc(sc_filled, 1)

            def weigh_self(t, i, g):
                if g == 0:
                    wait(pe, masked, t, lambda n: 12 * attends(n - 1) + 3 * i + 3)
                if i == 0 and g == 0:
                    wait(pe, copied, t, lambda n: 2 * outs(n))
                    wait(pe, vz_made, t, lambda n: 3 * attends(n))
                ab, h = g // 2, 4 * (g % 2) + i
                lo_keys = probs[:, (3 * i + g // 2) % RING, 256 * (g % 2):256 * (g % 2) + 256]
                hi_keys = probs[:, (3 * i + 2) % RING, 128 * g:128 * g + 128]
                nc.tensor.matmul(pself[0:VR, 256 * ab:256 * ab + 256],
                                 vz[:, t.n % 2, 0, ab, VR * h:VR * h + VR], lo_keys,
                                 start=(i == 0 and g == 0), stop=False)
                last = nc.tensor.matmul(pself[0:VR, 256 * ab + 128:256 * ab + 256],
                                        vz[:, t.n % 2, 1, ab, VR * h:VR * h + VR], hi_keys,
                                        start=False, stop=(i == 3 and g == 3))
                if g == G - 1:
                    last.then_inc(pv_done, 1)

            def weigh_cross(t, k):
                _, ip, gp = score_chunks()[12 + k]
                wait(pe, exp_done, t, lambda n: 16 * (n - 1) + 13 + k)
                if k == 0:
                    wait(pe, copied, t, lambda n: 2 * outs(n - 1))
                for x in range(2):
                    j = 2 * x + ip
                    last = nc.tensor.matmul(pcross[0:VR, 256 * gp:256 * gp + 256],
                                            vcz[:, (t.n - 1) % 2, gp, VR * j:VR * j + VR],
                                            probs[:, (12 + k) % RING, 256 * x:256 * x + 256],
                                            start=(k == 0 and x == 0), stop=(k == 3 and x == 1))
                last.then_inc(pv_done, 1)

            def ffn_prepare(t, k):
                z, pT2 = (t.n + 1) % 2, transposed_bank(t.n)
                if k == 1:
                    if t.n == -1:
                        pe.wait_ge(max_read, 16 * maxes(14))
                    wait(pe, xn2_made, t, ffn_preps)
                    for x in range(4):
                        last = nc.tensor.transpose(pT2[:, 128 * x:128 * x + 128], xn2[:, x, :], ident[:])
                    last.then_inc(xT2_filled, 1)
                if k == 3:
                    wait(pe, x_lo_made, t, ffn_preps)
                    if t.n == -1:
                        pe.wait_ge(w13_lo_made, 3)
                    for x in range(4):
                        for m, (xp, wp_) in enumerate(((x_hi, 0), (x_hi, 1), (x_lo, 0))):
                            last = nc.tensor.matmul(pT2[:, E * x:E * x + E], xp[:, z, 128 * x:128 * x + 128],
                                                    gw_parts[:, wp_, :], start=(m == 0), stop=(m == 2))
                    last.then_inc(gate_filled, 1)

            def hidden_tile(t, k):
                z = t.n % 2
                q = FK * (t.n % 2) + k
                if t.n == 0 and k == 0:
                    pe.wait_ge(w13_lo_made, 3)
                    pe.wait_ge(w13_hi_made, 4)
                if k == 0:
                    wait(pe, x_lo_made, t, lambda j: j + 1)
                if t.n == 0 and k == 1:
                    pe.wait_ge(combT_made, 1)
                wait(pe, silu_made, t, lambda j: FK * ffn_mains(j - 1) + k - 1)
                wait(pe, gated_made, t, lambda j: FK * ffn_mains(j - 1) + k - 1)
                for e, bank in ((0, ph1[q % 2]), (1, ph3[q % 2])):
                    for m, (wp_, x) in enumerate(((0, x_hi), (1, x_hi), (0, x_lo))):
                        last = nc.tensor.matmul(bank[:, :], w13_parts[:, wp_, e, 128 * k:128 * k + 128],
                                                x[:, z, :], start=(m == 0), stop=(m == 2))
                last.then_inc(h_filled, 1)
                if k == 0:
                    wait(pe, gate_steps, t, lambda j: GATE_STEPS * (j + 1))
                    for x in range(4):
                        last = nc.tensor.transpose(
                            transposed_bank(t.n - 1)[0:2 * E, 128 * x:128 * x + 128],
                            comb_parts[:, x, :, :].bitcast(F32).rearrange("p m e -> p (m e)"), ident[:])
                    last.then_inc(combT_filled, 1)

            def slot(t):
                if t.n == -2:
                    pe.wait_ge(fixed_in, 16)
                    pe.wait_ge(weights_in, n_weights)
                if t.n == 0:
                    pe.wait_ge(vc_made, 8)
                if has_prep(t.n):
                    wait(pe, xn_made, t, lambda n: preps(n))
                    wait_bank(t, "xT")
                    for k in range(4):
                        last = nc.tensor.transpose(psh[0][:, 128 * k:128 * k + 128], xn[:, k, :], ident[:])
                    last.then_inc(sh_filled, 1)
                if t.n == 0:
                    project(t, "q", wq)
                    project(t, "k", wk)
                for c, chunks in enumerate(max_steps(t.n)):
                    if has_out(t.n) and c == 0:
                        weigh_cross(t, 0)
                        weigh_cross(t, 1)
                    if has_attend(t.n):
                        score_chunk(t, c, *score_chunks()[c])
                    if has_out(t.n) and c in (1, 2):
                        weigh_cross(t, c + 1)
                    if has_prep(t.n) and c in (1, 2, 3) and (t.n != 0 or c == 3):
                        project(t, *(("q", wq), ("k", wk), ("qc", wcq))[c - 1])
                    for k, chunk in chunks:
                        max_chunk(t, k, *chunk)
                    if has_prep(t.n) and c == 4:
                        wait_bank(t, "v")
                        for k in range(4):
                            last = nc.tensor.matmul(psh[0][:, 128 * k:128 * k + 128], xnT[:, 128 * k:128 * k + 128],
                                                    wv[:], start=True, stop=True)
                        last.then_inc(sh_filled, 1)
                    if has_out(t.n) and c == 5:
                        wait(pe, copied, t, lambda n: 2 * outs(n))
                        for qt, kind in ((0, "o0"), (1, "o1")):
                            wait_bank(t, kind)
                            for x in range(2):
                                for ab in range(2):
                                    last = nc.tensor.transpose(
                                        psh[BANK[kind]][:, VR * (2 * x + ab):VR * (2 * x + ab) + VR],
                                        pcopy[:, x, 256 * ab + 128 * qt:256 * ab + 128 * qt + 128],
                                        ident[0:VR, 0:VR])
                            last.then_inc(sh_filled, 1)
                    if has_out(t.n) and c == 8:
                        wait(pe, y_made, t, lambda n: outs(n))
                        wait_bank(t, "yT")
                        for k in range(2):
                            last = nc.tensor.transpose(psh[1][:, 128 * k:128 * k + 128], y[:, k, :], ident[:])
                        last.then_inc(sh_filled, 1)
                    if has_out(t.n) and c == 10:
                        wait(pe, sh_emptied[1], t, emptied("yT"))
                        wait_bank(t, "proj")
                        for k in range(2):
                            last = nc.tensor.matmul(psh[0][:, 128 * k:128 * k + 128], yT[:, k, :], wp[:],
                                                    start=True, stop=True)
                        last.then_inc(sh_filled, 1)
                    if t.n == 16 and c in EARLY_AT:
                        hidden_tile(Slot(0), EARLY_AT.index(c))
                    if has_attend(t.n):
                        for i, g in weigh_at(c):
                            weigh_self(t, i, g)
                    if t.n == FIRST_PREP and c in STAGE_AT:
                        ffn_prepare(Slot(-1), STAGE_AT.index(c))
                    if has_max(t.n) and c == 11:
                        wait(pe, mparts_made, t, lambda n: 2 * maxes(n))
                        wait_bank(t, "mT")
                        for x in range(2):
                            for qt in range(2):
                                col = 256 * x + 128 * qt
                                last = nc.tensor.transpose(
                                    psh[1][0:32, col:col + 128],
                                    mparts[:, x, qt, :, :].bitcast(F32).rearrange("p h e -> p (h e)"), ident[:])
                        last.then_inc(sh_filled, 1)
                    if t.n == -2 and c == 3:
                        context_keys()
                    if t.n == -2 and c == 5:
                        context_values()

            attention_slots(pe, slot)
            pe.wait_ge(sh_emptied[0], attention_done)
            down = [(x, m) for x in range(4) for m in range(FK)]
            DOWN_AT = [0, 4, 8, 13, 18, 22, 27, 32, 36, 36]

            def ffn_slot(t):
                z = t.n % 2
                for k in range(FK):
                    if t.n <= 7:
                        if t.n > 0 or k >= len(EARLY_AT):
                            hidden_tile(t, k)
                    if t.n >= 1:
                        if k == 0:
                            wait(pe, x3_made, t, lambda j: ffn_downs(j - 1))
                            wait(pe, hidden_made, t, lambda j: (FK - 1) * ffn_mains(j - 2) + DOWN_AT[1])
                        if k == 1:
                            wait(pe, hidden_made, t, lambda j: (FK - 1) * ffn_mains(j - 1))
                            wait(pe, gated_made, t, lambda j: FK * ffn_mains(j - 1))
                        for x, m in down[DOWN_AT[k]:DOWN_AT[k + 1]]:
                            last = nc.tensor.matmul(py[:, C * x:C * x + C],
                                                    hidden[:, (t.n - 1) % 2, m, 128 * x:128 * x + 128], w2[:, m, :],
                                                    start=(m == 0), stop=(m == FK - 1))
                        if DOWN_AT[k] < DOWN_AT[k + 1] == len(down):
                            last.then_inc(down_filled, 1)
                    if t.n <= 7 and k < FK - 1:
                        if k == 0:
                            wait(pe, combT_made, t, lambda j: j + 1)
                        wait(pe, hidden_made, t, lambda j: (FK - 1) * ffn_mains(j - 1) + k - 1)
                        nc.tensor.matmul(pcb[k % 2][:, :], sel[:, k, :], combT[:, z, :], start=True,
                                         stop=True).then_inc(cb_filled, 1)
                    if t.n <= 6:
                        ffn_prepare(t, k)

            ffn_slots(pe, ffn_slot)


def host_constants():
    import numpy as np
    q, k = np.arange(128)[:, None], np.arange(128)[None, :]
    mask = np.where(k <= q, 0.0, -1e38).astype(np.float32)
    i = (np.arange(128) // 32) % 2
    sel = np.zeros((32, FK - 1, 128), np.float32)
    for t in range(FK - 1):
        for part in range(2):
            sel[16 * part + 2 * t, t, 0:HID] = 1.0
            sel[16 * part + 2 * t + 1, t, HID:] = 1.0
    halves = np.repeat(np.stack([np.arange(128) < 64, np.arange(128) >= 64], 1), D, 1).astype(np.float32)
    fixed = np.concatenate([np.eye(128, dtype=np.float32), np.stack([1 - i, i], 1).astype(np.float32), halves], 1)
    return {"fixed": fixed, "qmask": np.tile(mask, (1, 4)), "sel": sel.reshape(32, -1)}


def kernel(**inputs):
    import numpy as np
    import concourse.bacc as bacc
    from concourse.bass_utils import run_bass_kernel_spmd

    v = {k: np.asarray(x) for k, x in inputs.items()}
    w = {k: v["L0_xattn_" + k] for k in ("Wq", "Wk", "Wcq", "Wv", "Wp", "Wck", "Wcv",
                                         "bq", "bk", "bcq", "bck", "bv", "bcv", "bp")}
    arrays = {"w_all": np.concatenate([w[k] for k in ("Wq", "Wk", "Wcq", "Wv", "Wp")], 1),
              "wc_all": np.concatenate([w["Wck"], w["Wcv"]], 1),
              "bcol": np.stack([w[k] for k in ("bq", "bk", "bcq", "bck")], 1),
              "brow": np.concatenate([w[k] for k in ("bv", "bcv", "bp")]),
              "gates": np.concatenate([v["g_xattn"].reshape(1), v["g_ffn"].reshape(1)])}
    arrays["x"] = v["x"].reshape(B * T, C)
    arrays["ctxT"] = v["ctx_512"].reshape(B * TC, CC).T
    f = {k: v["L0_ffn_" + k] for k in ("gate_w", "w1", "w3", "w2", "sw1", "sw3", "sw2")}
    arrays["gwT"] = f["gate_w"].T
    for k in ("w1", "w3"):
        arrays[k + "T"] = f[k].reshape(E * HID, C).T
        arrays["s" + k + "T"] = f["s" + k].T
    arrays["w2T"] = f["w2"].transpose(0, 2, 1).reshape(E // 2, 2 * HID, C).transpose(1, 0, 2)
    arrays["sw2T"] = f["sw2"].T
    arrays.update(host_constants())

    nc = bacc.Bacc("TRN2", target_bir_lowering=False, num_devices=1)
    feeds, aps = {}, {}
    for k, x in arrays.items():
        feeds[f"in_{k}"] = np.ascontiguousarray(x)
        aps[k] = nc.dram_tensor(f"in_{k}", x.shape, mybir.dt.from_np(x.dtype), kind="ExternalInput").ap()
    out = nc.dram_tensor("out_0", (B * T, C), F32, kind="ExternalOutput").ap()
    block_program(nc, aps, out)
    r = run_bass_kernel_spmd(nc, [feeds], core_ids=[0])
    return r.results[0]["out_0"].reshape(B, T, C)
```
